# Optimizing a Trainium2 kernel written in Bass

```python
import numpy as np
import jax
import jax.numpy as jnp

def _softmax(x, axis=-1):
    return jax.nn.softmax(x, axis=axis)

def _gelu(x):
    return jax.nn.gelu(x, approximate=True)

def _silu(x):
    return jax.nn.silu(x)

def _sigmoid(x):
    return jax.nn.sigmoid(x)

def _layernorm(x, axis=-1, eps=1e-05):
    m = jnp.mean(x, axis=axis, keepdims=True)
    v = jnp.var(x, axis=axis, keepdims=True)
    return (x - m) / jnp.sqrt(v + eps)

def _scatter_add(tgt, idx, src, axis=0):
    return tgt.at[idx].add(src)

def _segment_sum(src, seg, n):
    return jax.ops.segment_sum(src, seg, n)
kernel_name = 'mk_conv_seq_d4_conv_nhwc512_r4_7338f1'

def setup_inputs(seed: int=0):
    np.random.seed(seed)
    _w = jnp.asarray

    def _rec_inputs():
        import jax
        import jax.numpy as jnp
        _gk = jax.random.key(seed)
        x = -0.0002928 + 1 * jax.random.normal(jax.random.fold_in(_gk, 1), (8, 32, 32, 128), jnp.float32)
        return x
    x = _rec_inputs()

    def _L0_conv_setup():
        import jax, jax.numpy as jnp
        import numpy as np
        NUM_HEADS = 8
        NUM_GROUPS = 16
        EPS = 1e-05

        def _group_norm(x, scale, bias):
            B, H, W, C = x.shape
            g = NUM_GROUPS
            xg = x.reshape(B, H, W, g, C // g)
            mean = jnp.mean(xg, axis=(1, 2, 4), keepdims=True)
            var = jnp.var(xg, axis=(1, 2, 4), keepdims=True)
            xn = (xg - mean) * jax.lax.rsqrt(var + EPS)
            xn = xn.reshape(B, H, W, C)
            return xn * scale + bias
        key = jax.random.key(seed)
        k1, k2, k3 = jax.random.split(key, 3)
        B, H, W, C = (8, 32, 32, 128)
        x = jax.random.normal(k1, (B, H, W, C), dtype=jnp.float32)
        gn_scale = jnp.ones((C,), dtype=jnp.float32)
        gn_bias = jnp.zeros((C,), dtype=jnp.float32)
        w_qkv = jax.random.normal(k2, (C, 3 * C), dtype=jnp.float32) * C ** (-0.5)
        w_out = jax.random.normal(k3, (C, C), dtype=jnp.float32) * C ** (-0.5)
        b_out = jnp.zeros((C,), dtype=jnp.float32)
        return {'x': x, 'gn_scale': gn_scale, 'gn_bias': gn_bias, 'w_qkv': w_qkv, 'w_out': w_out, 'b_out': b_out}
    _L0_conv_all = _L0_conv_setup()
    _L0_conv_in = {k: v for k, v in _L0_conv_all.items() if k in ('gn_scale', 'gn_bias', 'w_qkv', 'w_out', 'b_out')}
    del _L0_conv_all

    def _L1_conv_setup():
        import jax, jax.numpy as jnp
        import numpy as np
        GROUPS = 32
        EPS = 1e-05
        NUM_HEADS = 8
        HEAD_DIM = 16
        CHANNELS = 128

        def group_norm(x, scale, bias):
            b, h, w, c = x.shape
            xg = x.reshape(b, h, w, GROUPS, c // GROUPS)
            mean = jnp.mean(xg, axis=(1, 2, 4), keepdims=True)
            var = jnp.var(xg, axis=(1, 2, 4), keepdims=True)
            xg = (xg - mean) * jax.lax.rsqrt(var + EPS)
            return xg.reshape(b, h, w, c) * scale + bias
        key = jax.random.key(seed)
        ks = jax.random.split(key, 8)
        b, hs, ws, c = (8, 32, 32, CHANNELS)
        inner = NUM_HEADS * HEAD_DIM
        return {'x': jax.random.normal(ks[0], (b, hs, ws, c), dtype=jnp.float32), 't': jax.random.normal(ks[1], (b,), dtype=jnp.float32), 'gn_scale': jnp.ones((c,), dtype=jnp.float32), 'gn_bias': jnp.zeros((c,), dtype=jnp.float32), 'w_qkv': jax.random.normal(ks[2], (c, 3 * inner), dtype=jnp.float32) * 0.02, 'b_qkv': jnp.zeros((3 * inner,), dtype=jnp.float32), 'w_out': jax.random.normal(ks[3], (inner, c), dtype=jnp.float32) * 0.02, 'b_out': jnp.zeros((c,), dtype=jnp.float32)}
    _L1_conv_all = _L1_conv_setup()
    _L1_conv_in = {k: v for k, v in _L1_conv_all.items() if k in ('t', 'gn_scale', 'gn_bias', 'w_qkv', 'b_qkv', 'w_out', 'b_out')}
    del _L1_conv_all

    def _L2_conv_setup():
        import jax, jax.numpy as jnp
        import numpy as np
        B, H, W, C = (4, 16, 16, 128)
        LN_EPS = 0.001
        key = jax.random.key(seed)
        ks = jax.random.split(key, 10)
        s = 1.0 / np.sqrt(C)
        return {'x': jax.random.normal(ks[0], (B, H, W, C), dtype=jnp.float32), 'ln_g': jnp.ones((C,), jnp.float32), 'ln_b': jnp.zeros((C,), jnp.float32), 'Wq': jax.random.normal(ks[1], (C, C), jnp.float32) * s, 'bq': jnp.zeros((C,), jnp.float32), 'Wk': jax.random.normal(ks[2], (C, C), jnp.float32) * s, 'bk': jnp.zeros((C,), jnp.float32), 'Wv': jax.random.normal(ks[3], (C, C), jnp.float32) * s, 'bv': jnp.zeros((C,), jnp.float32), 'Wp': jax.random.normal(ks[4], (C, C), jnp.float32) * s, 'bp': jnp.zeros((C,), jnp.float32)}
    _L2_conv_all = _L2_conv_setup()
    _L2_conv_in = {k: v for k, v in _L2_conv_all.items() if k in ('ln_g', 'ln_b', 'Wq', 'bq', 'Wk', 'bk', 'Wv', 'bv', 'Wp', 'bp')}
    del _L2_conv_all

    def _L3_conv_setup():
        import jax, jax.numpy as jnp
        import numpy as np
        GROUPS = 32
        EPS = 1e-05

        def _group_norm(x, gamma, beta):
            B, H, W, C = x.shape
            xg = x.reshape(B, H, W, GROUPS, C // GROUPS)
            mean = jnp.mean(xg, axis=(1, 2, 4), keepdims=True)
            var = jnp.var(xg, axis=(1, 2, 4), keepdims=True)
            xg = (xg - mean) * jax.lax.rsqrt(var + EPS)
            return xg.reshape(B, H, W, C) * gamma + beta
        key = jax.random.key(seed)
        ks = jax.random.split(key, 10)
        B, H, W, C = (2, 16, 16, 128)
        s = 1.0 / np.sqrt(C)
        return {'x': jax.random.normal(ks[0], (B, H, W, C), dtype=jnp.float32), 'gamma': jnp.ones((C,), jnp.float32), 'beta': jnp.zeros((C,), jnp.float32), 'wq': jax.random.normal(ks[1], (C, C), jnp.float32) * s, 'bq': jnp.zeros((C,), jnp.float32), 'wk': jax.random.normal(ks[2], (C, C), jnp.float32) * s, 'bk': jnp.zeros((C,), jnp.float32), 'wv': jax.random.normal(ks[3], (C, C), jnp.float32) * s, 'bv': jnp.zeros((C,), jnp.float32), 'wp': jax.random.normal(ks[4], (C, C), jnp.float32) * s, 'bp': jnp.zeros((C,), jnp.float32)}
    _L3_conv_all = _L3_conv_setup()
    _L3_conv_in = {k: v for k, v in _L3_conv_all.items() if k in ('gamma', 'beta', 'wq', 'bq', 'wk', 'bk', 'wv', 'bv', 'wp', 'bp')}
    del _L3_conv_all
    return {'x': x, 'L0_conv_gn_scale': _L0_conv_in['gn_scale'], 'L0_conv_gn_bias': _L0_conv_in['gn_bias'], 'L0_conv_w_qkv': _L0_conv_in['w_qkv'], 'L0_conv_w_out': _L0_conv_in['w_out'], 'L0_conv_b_out': _L0_conv_in['b_out'], 'L1_conv_t': _L1_conv_in['t'], 'L1_conv_gn_scale': _L1_conv_in['gn_scale'], 'L1_conv_gn_bias': _L1_conv_in['gn_bias'], 'L1_conv_w_qkv': _L1_conv_in['w_qkv'], 'L1_conv_b_qkv': _L1_conv_in['b_qkv'], 'L1_conv_w_out': _L1_conv_in['w_out'], 'L1_conv_b_out': _L1_conv_in['b_out'], 'L2_conv_ln_g': _L2_conv_in['ln_g'], 'L2_conv_ln_b': _L2_conv_in['ln_b'], 'L2_conv_Wq': _L2_conv_in['Wq'], 'L2_conv_bq': _L2_conv_in['bq'], 'L2_conv_Wk': _L2_conv_in['Wk'], 'L2_conv_bk': _L2_conv_in['bk'], 'L2_conv_Wv': _L2_conv_in['Wv'], 'L2_conv_bv': _L2_conv_in['bv'], 'L2_conv_Wp': _L2_conv_in['Wp'], 'L2_conv_bp': _L2_conv_in['bp'], 'L3_conv_gamma': _L3_conv_in['gamma'], 'L3_conv_beta': _L3_conv_in['beta'], 'L3_conv_wq': _L3_conv_in['wq'], 'L3_conv_bq': _L3_conv_in['bq'], 'L3_conv_wk': _L3_conv_in['wk'], 'L3_conv_bk': _L3_conv_in['bk'], 'L3_conv_wv': _L3_conv_in['wv'], 'L3_conv_bv': _L3_conv_in['bv'], 'L3_conv_wp': _L3_conv_in['wp'], 'L3_conv_bp': _L3_conv_in['bp']}

def reference(x, L0_conv_gn_scale, L0_conv_gn_bias, L0_conv_w_qkv, L0_conv_w_out, L0_conv_b_out, L1_conv_t, L1_conv_gn_scale, L1_conv_gn_bias, L1_conv_w_qkv, L1_conv_b_qkv, L1_conv_w_out, L1_conv_b_out, L2_conv_ln_g, L2_conv_ln_b, L2_conv_Wq, L2_conv_bq, L2_conv_Wk, L2_conv_bk, L2_conv_Wv, L2_conv_bv, L2_conv_Wp, L2_conv_bp, L3_conv_gamma, L3_conv_beta, L3_conv_wq, L3_conv_bq, L3_conv_wk, L3_conv_bk, L3_conv_wv, L3_conv_bv, L3_conv_wp, L3_conv_bp):
    import jax
    import jax.numpy as jnp

    def _L0_conv_ref(x, gn_scale, gn_bias, w_qkv, w_out, b_out):
        import jax, jax.numpy as jnp
        import numpy as np
        NUM_HEADS = 8
        NUM_GROUPS = 16
        EPS = 1e-05

        def _group_norm(x, scale, bias):
            B, H, W, C = x.shape
            g = NUM_GROUPS
            xg = x.reshape(B, H, W, g, C // g)
            mean = jnp.mean(xg, axis=(1, 2, 4), keepdims=True)
            var = jnp.var(xg, axis=(1, 2, 4), keepdims=True)
            xn = (xg - mean) * jax.lax.rsqrt(var + EPS)
            xn = xn.reshape(B, H, W, C)
            return xn * scale + bias
        B, H, W, C = x.shape
        n = NUM_HEADS
        hd = C // n
        skip = x
        xn = _group_norm(x, gn_scale, gn_bias)
        qkv = jnp.einsum('bhwc,cd->bhwd', xn, w_qkv)
        qkv = qkv.reshape(B, H * W, n, 3 * hd)
        qkv = qkv.transpose(0, 2, 3, 1).reshape(B * n, 3 * hd, H * W)
        q, k, v = jnp.split(qkv, 3, axis=1)
        scores = jnp.einsum('bcq,bck->bqk', q, k) * hd ** (-0.5)
        scores = jax.nn.softmax(scores, axis=-1)
        o = jnp.einsum('bqk,bck->bqc', scores, v)
        o = o.reshape(B, n, H * W, hd).transpose(0, 2, 1, 3).reshape(B, H, W, C)
        out = jnp.einsum('bhwc,cd->bhwd', o, w_out) + b_out
        return out + skip

    def _L1_conv_ref(x, t, gn_scale, gn_bias, w_qkv, b_qkv, w_out, b_out):
        import jax, jax.numpy as jnp
        import numpy as np
        GROUPS = 32
        EPS = 1e-05
        NUM_HEADS = 8
        HEAD_DIM = 16
        CHANNELS = 128

        def group_norm(x, scale, bias):
            b, h, w, c = x.shape
            xg = x.reshape(b, h, w, GROUPS, c // GROUPS)
            mean = jnp.mean(xg, axis=(1, 2, 4), keepdims=True)
            var = jnp.var(xg, axis=(1, 2, 4), keepdims=True)
            xg = (xg - mean) * jax.lax.rsqrt(var + EPS)
            return xg.reshape(b, h, w, c) * scale + bias
        b, hs, ws, c = x.shape
        xn = group_norm(x, gn_scale, gn_bias)
        x_flat = xn.reshape(b, hs * ws, c)
        qkv = x_flat @ w_qkv + b_qkv
        qkv = qkv.reshape(b, hs * ws, NUM_HEADS, 3 * HEAD_DIM)
        q, k, v = jnp.split(qkv, 3, axis=-1)
        q = q / jnp.sqrt(jnp.float32(HEAD_DIM))
        q = q.transpose(0, 2, 1, 3)
        k = k.transpose(0, 2, 1, 3)
        v = v.transpose(0, 2, 1, 3)
        attn = jax.nn.softmax(jnp.einsum('bhqd,bhkd->bhqk', q, k), axis=-1)
        out = jnp.einsum('bhqk,bhkd->bhqd', attn, v)
        out = out.transpose(0, 2, 1, 3).reshape(b, hs * ws, NUM_HEADS * HEAD_DIM)
        h = out @ w_out + b_out
        h = h.reshape(b, hs, ws, c)
        return xn + h

    def _L2_conv_ref(x, ln_g, ln_b, Wq, bq, Wk, bk, Wv, bv, Wp, bp):
        import jax, jax.numpy as jnp
        import numpy as np
        B, H, W, C = (4, 16, 16, 128)
        LN_EPS = 0.001
        b, h_, w_, c = x.shape
        n = h_ * w_
        mu = jnp.mean(x, axis=-1, keepdims=True)
        var = jnp.var(x, axis=-1, keepdims=True)
        hn = (x - mu) * jax.lax.rsqrt(var + LN_EPS) * ln_g + ln_b
        hf = hn.reshape(b, n, c)
        q = hf @ Wq + bq
        k = hf @ Wk + bk
        v = hf @ Wv + bv
        scale = 1.0 / jnp.sqrt(jnp.asarray(c, x.dtype))
        scores = jnp.einsum('bqc,bkc->bqk', q, k) * scale
        attn = jax.nn.softmax(scores, axis=-1)
        o = jnp.einsum('bqk,bkc->bqc', attn, v)
        o = o @ Wp + bp
        return x + o.reshape(b, h_, w_, c)

    def _L3_conv_ref(x, gamma, beta, wq, bq, wk, bk, wv, bv, wp, bp):
        import jax, jax.numpy as jnp
        import numpy as np
        GROUPS = 32
        EPS = 1e-05

        def _group_norm(x, gamma, beta):
            B, H, W, C = x.shape
            xg = x.reshape(B, H, W, GROUPS, C // GROUPS)
            mean = jnp.mean(xg, axis=(1, 2, 4), keepdims=True)
            var = jnp.var(xg, axis=(1, 2, 4), keepdims=True)
            xg = (xg - mean) * jax.lax.rsqrt(var + EPS)
            return xg.reshape(B, H, W, C) * gamma + beta
        B, H, W, C = x.shape
        h_ = _group_norm(x, gamma, beta)
        q = jnp.einsum('bhwc,cd->bhwd', h_, wq) + bq
        k = jnp.einsum('bhwc,cd->bhwd', h_, wk) + bk
        v = jnp.einsum('bhwc,cd->bhwd', h_, wv) + bv
        q = q.reshape(B, H * W, C)
        k = k.reshape(B, H * W, C)
        v = v.reshape(B, H * W, C)
        scale = C ** (-0.5)
        attn = jax.nn.softmax(jnp.einsum('bqc,bkc->bqk', q, k) * scale, axis=-1)
        out = jnp.einsum('bqk,bkc->bqc', attn, v).reshape(B, H, W, C)
        proj = jnp.einsum('bhwc,cd->bhwd', out, wp) + bp
        return x + proj

    def _gn(v, G=32, eps=1e-05):
        B_, H_, W_, C_ = v.shape
        g = v.reshape(B_, H_, W_, G, C_ // G)
        m = jnp.mean(g, axis=(1, 2, 4), keepdims=True)
        s = jnp.var(g, axis=(1, 2, 4), keepdims=True)
        return ((g - m) / jnp.sqrt(s + eps)).reshape(v.shape)

    def _ln_c(v, eps=1e-06):
        m = jnp.mean(v, axis=-1, keepdims=True)
        s = jnp.var(v, axis=-1, keepdims=True)
        return (v - m) / jnp.sqrt(s + eps)

    def _ln_t(v, eps=1e-05):
        m = jnp.mean(v, axis=-1, keepdims=True)
        s = jnp.var(v, axis=-1, keepdims=True)
        return (v - m) / jnp.sqrt(s + eps)

    def _to_tokens(v):
        B_, H_, W_, C_ = v.shape
        return v.reshape(B_, H_ * W_, C_)

    def _from_tokens(t, like):
        return t.reshape(like.shape)
    x = _L0_conv_ref(x, L0_conv_gn_scale, L0_conv_gn_bias, L0_conv_w_qkv, L0_conv_w_out, L0_conv_b_out)
    x = _L1_conv_ref(x, L1_conv_t, L1_conv_gn_scale, L1_conv_gn_bias, L1_conv_w_qkv, L1_conv_b_qkv, L1_conv_w_out, L1_conv_b_out)
    x = _L2_conv_ref(x, L2_conv_ln_g, L2_conv_ln_b, L2_conv_Wq, L2_conv_bq, L2_conv_Wk, L2_conv_bk, L2_conv_Wv, L2_conv_bv, L2_conv_Wp, L2_conv_bp)
    x = _L3_conv_ref(x, L3_conv_gamma, L3_conv_beta, L3_conv_wq, L3_conv_bq, L3_conv_wk, L3_conv_bk, L3_conv_wv, L3_conv_bv, L3_conv_wp, L3_conv_bp)
    return x

_drawn_inputs = setup_inputs


def setup_inputs(seed=0):
    import zlib

    import numpy as np

    out = dict(_drawn_inputs(seed))
    spreads = {'L0_conv_gn_scale': (1.0, 0.2),
     'L0_conv_gn_bias': (0.0, 0.1),
     'L0_conv_b_out': (0.0, 0.1),
     'L1_conv_gn_scale': (1.0, 0.2),
     'L1_conv_gn_bias': (0.0, 0.1),
     'L1_conv_b_qkv': (0.0, 0.1),
     'L1_conv_b_out': (0.0, 0.1),
     'L2_conv_ln_g': (1.0, 0.2),
     'L2_conv_ln_b': (0.0, 0.1),
     'L2_conv_bq': (0.0, 0.774),
     'L2_conv_bk': (0.0, 0.8),
     'L2_conv_bv': (0.0, 0.1),
     'L2_conv_bp': (0.0, 0.1),
     'L3_conv_gamma': (1.0, 0.2),
     'L3_conv_beta': (0.0, 0.1),
     'L3_conv_bq': (0.0, 0.794),
     'L3_conv_bk': (0.0, 0.8),
     'L3_conv_bv': (0.0, 0.1),
     'L3_conv_bp': (0.0, 0.1)}
    factors = {'L1_conv_w_qkv': 3.841}
    for name, (base, spread) in spreads.items():
        noise = np.random.default_rng([zlib.crc32(name.encode()), seed]).standard_normal(out[name].shape)
        drawn = base * np.exp(spread * noise) if base else spread * noise
        out[name] = jnp.asarray(drawn.astype(out[name].dtype))
    for name, factor in factors.items():
        out[name] = (out[name] * factor).astype(out[name].dtype)
    return out
```

```python
from contextlib import ExitStack

import concourse.bass as bass
from concourse import mybir

P = 128
IMAGES, TOKENS, CHANNELS = 8, 1024, 128
PAIR = 2
STAGES = 8
HEAD_STAGES = 4
HEADS, HD = 8, 16
GROUP = 4
KT = TOKENS // P
HALF = TOKENS // 2
N_GROUPS = HEAD_STAGES * HEADS // GROUP
SLOTS = 2 * KT
TILES = GROUP * KT
TILE_SLOTS = 14
PROB_RING = 3
HEAD_SCALE = float(HD) ** -0.5
FULL_SCALE = float(CHANNELS) ** -0.5
GN_EPS, LN_EPS = 1e-5, 1e-3

Q_PART = [0, 0, 0, 1, 1, 2]
K_PART = [0, 1, 2, 0, 1, 0]
STACK = HD * len(Q_PART)
SHIFT = 2

F32, BF16 = mybir.dt.float32, mybir.dt.bfloat16
ALU = mybir.AluOpType
ACT = mybir.ActivationFunctionType
AX_X = mybir.AxisListType.X

GN_STEPS, LN_STEPS = 8, 4
GN_STAGES = [0, 1, 2, 3, 6, 7]
LN_STAGES = [4, 5]


def projections(s):
    return [(n, s) for n in ("k0", "k1", "q0", "q1", "v0", "v1")]


def head_chunks():
    at = {}

    def put(g, slot, *names):
        at.setdefault((g, slot), []).extend(names)

    for g in range(N_GROUPS):
        s = g // 2
        if g % 2 == 0:
            if s >= 1:
                put(g, 2, ("out0", s - 1))
                put(g, 3, ("out1", s - 1))
            if s == 0:
                put(g, 2, ("in0", 1))
                put(g, 3, ("in1", 1))
            if s + 1 < HEAD_STAGES:
                put(g, 4, ("stats", s + 1))
                put(g, 5, ("gn1", s + 1))
                put(g, 6, ("gn2", s + 1))
                put(g, 7, ("apply", s + 1))
                for i, n in enumerate(projections(s + 1)):
                    put(g, 8 + i, n)
            else:
                put(g, 5, ("turn0", s + 1))
                put(g, 6, ("turn1", s + 1))
                put(g, 7, ("ln", s + 1))
                put(g, 9, ("back0", s + 1))
                put(g, 10, ("back1", s + 1))
        elif s + 1 == HEAD_STAGES:
            for i, n in enumerate(projections(s + 1)):
                put(g, 2 * i, n)
        if g + 1 < N_GROUPS:
            put(g, TILE_SLOTS, ("shift", g + 1))
    return at


def full_chunks():
    at = {}
    for s in range(HEAD_STAGES, STAGES):
        for n, t in (("out0", 0), ("out1", 1)):
            at.setdefault((s, t), []).append((n, s - 1))
        if s == STAGES - 1:
            at.setdefault((s, 3), []).append(("turned0", s - 1))
            at.setdefault((s, 4), []).append(("turned1", s - 1))
            continue
        if s + 1 in LN_STAGES:
            for n, t in (("turn0", 2), ("turn1", 2), ("ln", 3), ("back0", 4), ("back1", 4)):
                at.setdefault((s, t), []).append((n, s + 1))
        else:
            for n, t in (("stats", 2), ("gn1", 3), ("gn2", 3), ("apply", 4)):
                at.setdefault((s, t), []).append((n, s + 1))
        for i, n in enumerate(projections(s + 1)):
            at.setdefault((s, 5 + i // 2), []).append(n)
    return at


FIRST = [("in0", 0), ("in1", 0), ("stats", 0), ("gn1", 0), ("gn2", 0), ("apply", 0), *projections(0)]
LAST = [(n, STAGES - 1) for n in ("out0", "out1", "turned0", "turned1")]
NO_BANK = ("stats", "apply", "ln")


def bank_uses(heads, fulls):
    order = list(FIRST) + [("shift", 0)]
    for g in range(N_GROUPS):
        for i in range(SLOTS):
            order += heads.get((g, i), [])
    for s in range(HEAD_STAGES, STAGES):
        for t in range(KT):
            order += fulls.get((s, t), [])
    order += LAST
    return {n: i for i, n in enumerate(x for x in order if x[0] not in NO_BANK)}


def tiles_of_slot(g, slot):
    if g >= N_GROUPS or slot >= TILE_SLOTS:
        return range(0)
    return range(-(-TILES * slot // TILE_SLOTS), -(-TILES * (slot + 1) // TILE_SLOTS))


def attention_blocks(nc, x, weights, vectors, v_bias, averages, out):
    heads, fulls = head_chunks(), full_chunks()
    use = bank_uses(heads, fulls)

    with ExitStack() as ctx:
        def sb(name, shape, dt=F32):
            return ctx.enter_context(nc.sbuf_tensor(name, shape, dt))

        def psum(name, shape, dt=F32):
            return ctx.enter_context(nc.psum_tensor(name, shape, dt))

        def sem(name):
            s = ctx.enter_context(nc.semaphore(name))
            loop_sems.append(s)
            return s

        loop_sems = []

        N_W = weights.shape[1]
        w = sb("w", [P, N_W])
        vec = sb("vec", [P, vectors.shape[1]])
        qbias = sb("qbias", [P, 4])
        vb = sb("vb", [P, 4, CHANNELS])
        avg = sb("avg", [P, 4 * P])
        minus_half = sb("minus_half", [P, KT])
        xin = sb("xin", [P, PAIR, KT, CHANNELS])
        xT = sb("xT", [P, PAIR, TOKENS])
        hT = sb("hT", [P, PAIR, TOKENS])
        xtok = sb("xtok", [P, KT, CHANNELS])
        q32 = sb("q32", [P, PAIR, TOKENS])
        k32 = sb("k32", [P, PAIR, TOKENS])
        q_parts = sb("q_parts", [P, 3, TOKENS], BF16)
        k_parts = sb("k_parts", [P, 3, TOKENS], BF16)
        rest = sb("rest", [P, HALF])
        q_stack = sb("q_stack", [P, PAIR * HEADS * TOKENS], BF16)
        k_stack = sb("k_stack", [P, PAIR * HEADS * TOKENS], BF16)
        v_heads = sb("v_heads", [P, PAIR, KT, HEADS, 2 * HD])
        v_full = sb("v_full", [P, PAIR, KT, CHANNELS])
        probs = sb("probs", [P, PROB_RING, GROUP, HALF])
        o_raw = sb("o_raw", [P, 2, HALF])
        o_sum = sb("o_sum", [P, 2, HALF])
        o_inv = sb("o_inv", [P, 2, HALF])
        oT = sb("oT", [P, 2, TOKENS])
        neg_max = sb("neg_max", [P, 2, TILES])
        shift_parts = sb("shift_parts", [TILES, 2, P], BF16)
        stats = sb("stats", [P, KT, nc.vector.BN_STATS_DIM])
        mv = sb("mv", [P, KT, 2])
        gmean = sb("gmean", [P, 1])
        dev = sb("dev", [P, 1])
        var_in = sb("var_in", [P, 1])
        var_eps = sb("var_eps", [P, KT])
        rstd = sb("rstd", [P, KT])
        gscale = sb("gscale", [P, 1])
        gshift = sb("gshift", [P, 2])
        neg_max1 = sb("neg_max1", [P, 4])
        sum1 = sb("sum1", [P, 4])
        inv1 = sb("inv1", [P, 4])
        p_full = probs[:, 0, :, :].rearrange("p a b -> p (a b)").rearrange("p (n k) -> p n k", n=2)
        pT_full = q_stack[:, :].bitcast(F32).rearrange("p (k q) -> p k q", k=KT)
        qs = q_stack[:, :].rearrange("p (i h t) -> p i h t", i=PAIR, h=HEADS)
        ks = k_stack[:, :].rearrange("p (i h t) -> p i h t", i=PAIR, h=HEADS)

        ident = avg[:, 3 * P:4 * P]
        group_avg = {0: avg[:, 0:P], 1: avg[:, P:2 * P], 3: avg[:, P:2 * P]}

        def w_of(layer, n):
            return w[:, (3 * layer + n) * P:(3 * layer + n + 1) * P]

        def w_out(layer, g=0):
            n = 12 + (2 * layer + g if layer < 2 else 2 + layer)
            return w[:, n * P:(n + 1) * P]

        def vec_of(layer, n):
            return vec[:, 5 * layer + n:5 * layer + n + 1]

        scores = [psum(f"scores{i}", [P, TOKENS]) for i in range(2)]
        turned = psum("turned", [P, 2, HALF])
        outs = psum("outs", [P, HALF])
        bank = psum("bank", [P, HALF])

        scratch = {n: nc.dram_tensor(f"{n}_scratch", [3, P, TOKENS], BF16, kind="Internal").ap()
                   for n in "qk"}

        setup_loads = ctx.enter_context(nc.semaphore("setup_loads"))
        setup_done = ctx.enter_context(nc.semaphore("setup_done"))
        image_loaded = sem("image_loaded")
        bank_full = sem("bank_full")
        bank_read = sem("bank_read")
        gn_step = sem("gn_step")
        ln_step = sem("ln_step")
        rstd_ready = sem("rstd_ready")
        h_ready = sem("h_ready")
        split = sem("split")
        parts_out = {n: sem(f"{n}_parts_out") for n in "qk"}
        stacked = {n: sem(f"{n}_stacked") for n in "qk"}
        tile_full = sem("tile_full")
        tile_max = sem("tile_max")
        shift_hi = sem("shift_hi")
        shift_in = sem("shift_in")
        turned_full = sem("turned_full")
        exp_done = sem("exp_done")
        pv_done = sem("pv_done")
        o_copied = sem("o_copied")
        o_spread = sem("o_spread")
        o_inverse = sem("o_inverse")
        o_ready = sem("o_ready")
        f_scores = sem("f_scores")
        f_max = sem("f_max")
        f_exp = sem("f_exp")
        f_inv = sem("f_inv")
        f_norm = sem("f_norm")
        f_turned = sem("f_turned")
        f_copied_lo = sem("f_copied_lo")
        f_copied_hi = sem("f_copied_hi")
        f_pv = sem("f_pv")
        f_out = sem("f_out")
        y_stored = sem("y_stored")

        with nc.Block() as block:
            @block.sync
            def _(sp):
                sp.dma_start(avg[:, :], averages).then_inc(setup_loads, 16)
                sp.dma_start(w[:, :], weights).then_inc(setup_loads, 16)
                sp.dma_start(vec[:, :], vectors).then_inc(setup_loads, 16)
                sp.dma_start(vb[:, :, :], v_bias.partition_broadcast(P)).then_inc(setup_loads, 16)
                sp.wait_ge(setup_loads, 64)

            @block.vector
            def _(dve):
                nc.vector.memset(v_heads[:, :, :, :, HD:2 * HD], 1.0)
                nc.vector.memset(minus_half[:, :], -0.5)
                nc.vector.memset(ks[STACK:STACK + SHIFT, :, :, :], 1.0)
                dve.wait_ge(setup_loads, 64)
                for layer in range(4):
                    scale = 1.0 if layer < 2 else FULL_SCALE
                    last = nc.vector.tensor_scalar(qbias[:, layer:layer + 1], vec_of(layer, 2), scale,
                                                   None, ALU.mult)
                last.then_inc(setup_done, 1)
                dve.wait_ge(setup_done, 1)
        nc.all_engine_barrier()

        with nc.Fori(0, IMAGES // PAIR) as step:
            with nc.Block() as block:
                @block.sync
                def _(sp):
                    for i in range(PAIR):
                        image = x[bass.ds(step * PAIR + i, 1)].rearrange("o (p j) c -> (o p) j c", j=KT)
                        sp.dma_start(xin[:, i, :, :], image).then_inc(image_loaded, 16)

                    def stack(s):
                        for i, (n, parts) in enumerate((("k", k_parts), ("q", q_parts))):
                            sp.wait_ge(split, 16 * s + 8 * (i + 1))
                            sp.dma_start(scratch[n].rearrange("j p t -> p j t"), parts[:, :, :]
                                         ).then_inc(parts_out[n], 16)
                        for n, to, which in (("k", ks, K_PART), ("q", qs, Q_PART)):
                            sp.wait_ge(parts_out[n], 16 * (s + 1))
                            for j, part in enumerate(which):
                                sp.dma_start(to[HD * j:HD * (j + 1), s % 2, :, :],
                                             scratch[n][part].rearrange("(h r) t -> r h t", r=HD)
                                             ).then_inc(stacked[n], 16)

                    def shift(g):
                        first = GROUP * (g % 2)
                        sp.wait_ge(bank_read, use["shift", g] + 1)
                        for j in range(SHIFT):
                            row = qs[STACK + j:STACK + j + 1, (g // 2) % 2, first:first + GROUP, :]
                            sp.dma_start(row.rearrange("o h (n q) -> o (h n) q", n=KT),
                                         shift_parts[:, j, :]).then_inc(shift_in, 16)

                    stack(0)
                    shift(0)
                    for g in range(N_GROUPS):
                        if g % 2 == 0 and g // 2 + 1 < HEAD_STAGES:
                            stack(g // 2 + 1)
                        if g + 1 < N_GROUPS:
                            shift(g + 1)
                    for i in range(PAIR):
                        sp.wait_ge(bank_read, use["turned1", STAGES - PAIR + i] + 1)
                        image = out[bass.ds(step * PAIR + i, 1)].rearrange("o (p j) c -> (o p) j c", j=KT)
                        sp.dma_start(image, xin[:, i, :, :]).then_inc(y_stored, 16)
                    sp.wait_ge(y_stored, 16 * PAIR)

                @block.gpsimd
                def _(pool):
                    def inverse_root(s):
                        n = KT if s in LN_STAGES else 1
                        if s in LN_STAGES:
                            pool.wait_ge(ln_step, LN_STEPS * LN_STAGES.index(s) + 3)
                        else:
                            pool.wait_ge(bank_read, use["gn2", s] + 1)
                        nc.gpsimd.tensor_tensor(rstd[:, 0:n], var_eps[:, 0:n], minus_half[:, 0:n],
                                                ALU.pow).then_inc(rstd_ready, 1)

                    def split_parts(s):
                        done = 16 * s
                        for i, (whole, parts) in enumerate(((k32, k_parts), (q32, q_parts))):
                            for t in range(2):
                                cols = slice(HALF * t, HALF * (t + 1))
                                pool.wait_ge(bank_read, use["kq"[i] + "01"[t], s] + 1)
                                nc.gpsimd.tensor_copy(parts[:, 0, cols], whole[:, s % 2, cols]
                                                      ).then_inc(split, 1)
                                pool.wait_ge(split, done + 1)
                                nc.gpsimd.tensor_tensor(rest[:, :], whole[:, s % 2, cols],
                                                        parts[:, 0, cols], ALU.subtract
                                                        ).then_inc(split, 1)
                                pool.wait_ge(split, done + 2)
                                nc.gpsimd.tensor_copy(parts[:, 1, cols], rest[:, :]).then_inc(split, 1)
                                pool.wait_ge(split, done + 3)
                                nc.gpsimd.tensor_tensor(parts[:, 2, cols], rest[:, :],
                                                        parts[:, 1, cols], ALU.subtract
                                                        ).then_inc(split, 1)
                                done += 4
                                pool.wait_ge(split, done)

                    def normalise(g, half):
                        if g >= 2:
                            pool.wait_ge(bank_full, use["out1", g // 2 - 1] + 1)
                        pool.wait_ge(o_inverse, 2 * g + half + 1)
                        nc.gpsimd.tensor_tensor(oT[:, g % 2, HALF * half:HALF * (half + 1)],
                                                o_raw[:, half, :], o_inv[:, half, :], ALU.mult
                                                ).then_inc(o_ready, 1)

                    inverse_root(0)
                    split_parts(0)
                    for g in range(N_GROUPS):
                        s = g // 2
                        if g >= 1:
                            normalise(g - 1, 1)
                        if g % 2 == 0 and s + 1 <= HEAD_STAGES:
                            inverse_root(s + 1)
                        if g % 2 == 0 and s + 1 < HEAD_STAGES:
                            split_parts(s + 1)
                        normalise(g, 0)
                    normalise(N_GROUPS - 1, 1)
                    for s in range(HEAD_STAGES + 1, STAGES):
                        inverse_root(s)

                @block.scalar
                def _(act):
                    def chunk(name, s):
                        kind = name.rstrip("01")
                        half = int(name[-1]) if name[-1] in "01" else 0
                        layer, i = s // 2, s % 2
                        cols = slice(HALF * half, HALF * (half + 1))
                        tiles = slice(half * KT // 2, (half + 1) * KT // 2)
                        if kind == "in":
                            act.wait_ge(bank_full, use[name, s] + 1)
                            nc.scalar.copy(xT[:, i, cols], bank[:, :]).then_inc(bank_read, 1)
                        elif kind == "turn":
                            act.wait_ge(bank_full, use[name, s] + 1)
                            nc.scalar.copy(xtok[:, tiles, :], bank[:, :].rearrange(
                                "p (j c) -> p j c", c=CHANNELS)).then_inc(bank_read, 1)
                        elif kind == "back":
                            act.wait_ge(bank_full, use[name, s] + 1)
                            nc.scalar.activation(hT[:, i, cols], bank[:, :], ACT.Identity,
                                                 bias=vec_of(layer, 1), scale=vec_of(layer, 0)
                                                 ).then_inc(bank_read, 1)
                        elif kind in ("q", "k"):
                            act.wait_ge(bank_full, use[name, s] + 1)
                            to, bias, scale = (k32, vec_of(layer, 3), 1.0) if kind == "k" else (
                                q32, qbias[:, layer:layer + 1], 1.0 if layer < 2 else FULL_SCALE)
                            nc.scalar.activation(to[:, i, cols], bank[:, :], ACT.Identity, bias=bias,
                                                 scale=scale).then_inc(bank_read, 1)
                        elif kind == "shift":
                            if s >= 1:
                                act.wait_ge(shift_in, 32 * s)
                            act.wait_ge(bank_full, use[name, s] + 1)
                            nc.scalar.copy(shift_parts[:, 0, :], bank[0:TILES, 0:P]).then_inc(shift_hi, 1)
                        elif kind == "turned":
                            act.wait_ge(bank_full, use[name, s] + 1)
                            nc.scalar.copy(xin[:, i, tiles, :], bank[:, :].rearrange(
                                "p (j c) -> p j c", c=CHANNELS)).then_inc(bank_read, 1)

                    def copy_outputs(n):
                        act.wait_ge(pv_done, KT * (n + 1))
                        if n >= 2:
                            act.wait_ge(o_ready, n - 1)
                        nc.scalar.copy(o_raw[:, n % 2, :], outs[:, :]).then_inc(o_copied, 1)

                    def exp(u, h):
                        t = GROUP * u + h
                        if h == 0 and u >= PROB_RING:
                            act.wait_ge(pv_done, u - PROB_RING + 1)
                        act.wait_ge(turned_full, t + 1)
                        nc.scalar.activation(probs[:, u % PROB_RING, h, :], turned[:, t % 2, :], ACT.Exp,
                                             scale=HEAD_SCALE).then_inc(exp_done, 1)

                    for c in FIRST + [("shift", 0)]:
                        chunk(*c)
                    for g in range(N_GROUPS):
                        for slot in range(SLOTS):
                            u = SLOTS * g + slot
                            exp(u, 0)
                            if u % KT == 1 and u > KT:
                                copy_outputs(u // KT - 1)
                            for c in heads.get((g, slot), []):
                                chunk(*c)
                            for h in range(1, GROUP):
                                exp(u, h)
                    copy_outputs(2 * N_GROUPS - 1)

                    def full_exp(n):
                        act.wait_ge(f_max, n + 1)
                        if n >= 2:
                            act.wait_ge(f_turned, n - 1)
                        nc.scalar.activation(p_full[:, n % 2, :], scores[n % 2][:, :], ACT.Exp,
                                             bias=neg_max1[:, n % 4:n % 4 + 1],
                                             accum_out=sum1[:, n % 4:n % 4 + 1]).then_inc(f_exp, 1)

                    def full_out(m, half):
                        act.wait_ge(f_pv, 2 * m + half + 1)
                        nc.scalar.copy(oT[:, 0, HALF * half:HALF * (half + 1)], outs[:, :]
                                       ).then_inc(f_out, 1)

                    for m, s in enumerate(range(HEAD_STAGES, STAGES)):
                        full_exp(KT * m)
                        full_exp(KT * m + 1)
                        for t in range(KT):
                            n = KT * m + t
                            act.wait_ge(f_turned, n + 1)
                            if t == 0 and m >= 1:
                                act.wait_ge(f_pv, 2 * m)
                            nc.scalar.copy(pT_full[:, 0:KT // 2, P * t:P * (t + 1)],
                                           turned[:, 0, :].rearrange("p (k q) -> p k q", q=P)
                                           ).then_inc(f_copied_lo, 1)
                            if t + 2 < KT:
                                full_exp(n + 2)
                            for c in fulls.get((s, t), []):
                                chunk(*c)
                        for half in range(2):
                            full_out(m, half)
                    for c in LAST:
                        chunk(*c)

                @block.vector
                def _(dve):
                    def chunk(name, s):
                        kind = name.rstrip("01") if name[-1] in "01" else name
                        half = int(name[-1]) if name[-1] in "01" else 0
                        layer, i = s // 2, s % 2
                        cols = slice(HALF * half, HALF * (half + 1))
                        if name in ("gn1", "gn2"):
                            kind = name
                        if kind in ("stats", "gn1", "gn2", "apply"):
                            step0 = GN_STEPS * GN_STAGES.index(s)
                        if kind == "stats":
                            if s < 2:
                                dve.wait_ge(bank_read, use["in1", s] + 1)
                            else:
                                dve.wait_ge(bank_read, use["out1", s - 2] + 1)
                            for t in range(2):
                                nc.vector.bn_stats(stats[:, t, :], xT[:, i, HALF * t:HALF * (t + 1)]
                                                   ).then_inc(gn_step, 1)
                            dve.wait_ge(gn_step, step0 + 2)
                            nc.vector.bn_aggr(mv[:, 0, :], stats[:, 0:2, :]).then_inc(gn_step, 1)
                        elif kind == "gn1":
                            dve.wait_ge(bank_full, use[name, s] + 1)
                            nc.vector.tensor_copy(gmean[:, :], bank[:, 0:1]).then_inc(bank_read, 1)
                            dve.wait_ge(bank_read, use[name, s] + 1)
                            nc.vector.tensor_tensor(dev[:, :], mv[:, 0, 0:1], gmean[:, :], ALU.subtract
                                                    ).then_inc(gn_step, 1)
                            dve.wait_ge(gn_step, step0 + 4)
                            nc.vector.scalar_tensor_tensor(var_in[:, :], dev[:, :], dev[:, :],
                                                           mv[:, 0, 1:2], ALU.mult, ALU.add
                                                           ).then_inc(gn_step, 1)
                        elif kind == "gn2":
                            dve.wait_ge(bank_full, use[name, s] + 1)
                            nc.vector.tensor_scalar(var_eps[:, 0:1], bank[:, 0:1], GN_EPS, None,
                                                    ALU.add).then_inc(bank_read, 1)
                        elif kind == "apply":
                            dve.wait_ge(rstd_ready, s + 1)
                            nc.vector.tensor_tensor(gscale[:, :], rstd[:, 0:1], vec_of(layer, 0),
                                                    ALU.mult).then_inc(gn_step, 1)
                            dve.wait_ge(gn_step, step0 + 6)
                            nc.vector.tensor_tensor(gshift[:, 0:1], gmean[:, :], gscale[:, :], ALU.mult
                                                    ).then_inc(gn_step, 1)
                            dve.wait_ge(gn_step, step0 + 7)
                            nc.vector.tensor_tensor(gshift[:, 1:2], vec_of(layer, 1), gshift[:, 0:1],
                                                    ALU.subtract).then_inc(gn_step, 1)
                            dve.wait_ge(gn_step, step0 + 8)
                            nc.vector.tensor_scalar(hT[:, i, :], xT[:, i, :], gscale[:, :],
                                                    gshift[:, 1:2], ALU.mult, ALU.add
                                                    ).then_inc(h_ready, 1)
                        elif kind == "ln":
                            step0 = LN_STEPS * LN_STAGES.index(s)
                            dve.wait_ge(bank_read, use["turn1", s] + 1)
                            for j in range(KT):
                                last = nc.vector.bn_stats(stats[:, j, :], xtok[:, j, :])
                            last.then_inc(ln_step, 1)
                            dve.wait_ge(ln_step, step0 + 1)
                            for j in range(KT):
                                last = nc.vector.bn_aggr(mv[:, j, :], stats[:, j, :])
                            last.then_inc(ln_step, 1)
                            dve.wait_ge(ln_step, step0 + 2)
                            nc.vector.tensor_scalar(var_eps[:, :], mv[:, :, 1], LN_EPS, None, ALU.add
                                                    ).then_inc(ln_step, 1)
                            dve.wait_ge(rstd_ready, s + 1)
                            for j in range(KT):
                                last = nc.vector.tensor_scalar(xtok[:, j, :], xtok[:, j, :],
                                                               mv[:, j, 0:1], rstd[:, j:j + 1],
                                                               ALU.subtract, ALU.mult)
                            last.then_inc(ln_step, 1)
                        elif kind == "v":
                            dve.wait_ge(bank_full, use[name, s] + 1)
                            tiles = slice(half * KT // 2, (half + 1) * KT // 2)
                            bias = vb[:, layer, :].unsqueeze(1).to_broadcast([P, KT // 2, CHANNELS])
                            src = bank[:, :].rearrange("p (j c) -> p j c", c=CHANNELS)
                            if s < HEAD_STAGES:
                                for j in range(KT // 2):
                                    last = nc.vector.tensor_tensor(
                                        v_heads[:, i, half * KT // 2 + j, :, 0:HD],
                                        bank[:, P * j:P * (j + 1)].rearrange("p (h d) -> p h d", h=HEADS),
                                        vb[:, layer, :].rearrange("p (h d) -> p h d", h=HEADS), ALU.add)
                                last.then_inc(bank_read, 1)
                            else:
                                nc.vector.tensor_tensor(v_full[:, i, tiles, :], src, bias, ALU.add
                                                        ).then_inc(bank_read, 1)
                        elif kind == "shift":
                            dve.wait_ge(shift_hi, s + 1)
                            nc.vector.tensor_tensor(shift_parts[:, 1, :], bank[0:TILES, 0:P],
                                                    shift_parts[:, 0, :], ALU.subtract
                                                    ).then_inc(bank_read, 1)
                        elif kind == "out":
                            skip = hT if layer == 1 else xT
                            dve.wait_ge(bank_full, use[name, s] + 1)
                            nc.vector.scalar_tensor_tensor(xT[:, i, cols], bank[:, :], vec_of(layer, 4),
                                                           skip[:, i, cols], ALU.add, ALU.add
                                                           ).then_inc(bank_read, 1)

                    def tile_maximum(g, n):
                        dve.wait_ge(tile_full, TILES * g + n + 1)
                        nc.vector.tensor_reduce(neg_max[:, g % 2, n:n + 1],
                                                scores[n % 2][:, :], AX_X, ALU.max, negate=True
                                                ).then_inc(tile_max, 1)

                    def spread_sums(n):
                        dve.wait_ge(o_copied, n + 1)
                        if n >= 2:
                            dve.wait_ge(o_ready, n - 1)
                        rows = [HD] * HD + list(range(HD, 2 * HD))
                        nc.vector.stream_shuffle(o_sum[:, n % 2, :], o_raw[:, n % 2, :], rows
                                                 ).then_inc(o_spread, 1)
                        dve.wait_ge(o_spread, n + 1)
                        nc.vector.reciprocal(o_inv[:, n % 2, :], o_sum[:, n % 2, :]
                                             ).then_inc(o_inverse, 1)

                    for c in FIRST:
                        chunk(*c)
                    for n in range(TILES):
                        tile_maximum(0, n)
                    chunk("shift", 0)
                    for g in range(N_GROUPS):
                        for slot in range(SLOTS):
                            u = SLOTS * g + slot
                            if u % KT == 1 and u > KT:
                                spread_sums(u // KT - 1)
                            for c in heads.get((g, slot), []):
                                chunk(*c)
                            for n in tiles_of_slot(g + 1, slot):
                                tile_maximum(g + 1, n)
                    spread_sums(2 * N_GROUPS - 1)

                    def full_max(n):
                        dve.wait_ge(f_scores, n + 1)
                        nc.vector.tensor_reduce(neg_max1[:, n % 4:n % 4 + 1], scores[n % 2][:, :], AX_X,
                                                ALU.max, negate=True).then_inc(f_max, 1)

                    for m, s in enumerate(range(HEAD_STAGES, STAGES)):
                        full_max(KT * m)
                        full_max(KT * m + 1)
                        for t in range(KT):
                            n = KT * m + t
                            dve.wait_ge(f_exp, n + 1)
                            nc.vector.reciprocal(inv1[:, n % 4:n % 4 + 1], sum1[:, n % 4:n % 4 + 1]
                                                 ).then_inc(f_inv, 1)
                            dve.wait_ge(f_inv, n + 1)
                            nc.vector.tensor_scalar(p_full[:, n % 2, :], p_full[:, n % 2, :],
                                                    inv1[:, n % 4:n % 4 + 1], None, ALU.mult
                                                    ).then_inc(f_norm, 1)
                            if t + 2 < KT:
                                full_max(n + 2)
                            dve.wait_ge(f_turned, n + 1)
                            if t == 0 and m >= 1:
                                dve.wait_ge(f_pv, 2 * m)
                            nc.vector.tensor_copy(pT_full[:, KT // 2:KT, P * t:P * (t + 1)],
                                                  turned[:, 1, :].rearrange("p (k q) -> p k q", q=P)
                                                  ).then_inc(f_copied_hi, 1)
                            for c in fulls.get((s, t), []):
                                chunk(*c)
                    for c in LAST:
                        chunk(*c)

                @block.tensor
                def _(pe):
                    def chunk(name, s):
                        kind = name if name in ("gn1", "gn2") else name.rstrip("01")
                        if kind in NO_BANK:
                            return
                        half = int(name[-1]) if name[-1] in "01" else 0
                        layer, i = s // 2, s % 2
                        cols = slice(HALF * half, HALF * (half + 1))
                        if use[name, s] >= 1:
                            pe.wait_ge(bank_read, use[name, s])
                        if kind == "in":
                            pe.wait_ge(image_loaded, 16 * PAIR)
                            for j in range(KT // 2):
                                last = nc.tensor.transpose(bank[:, P * j:P * (j + 1)],
                                                           xin[:, i, half * KT // 2 + j, :], ident)
                        elif kind == "gn1":
                            pe.wait_ge(gn_step, GN_STEPS * GN_STAGES.index(s) + 3)
                            last = nc.tensor.matmul(bank[:, 0:1], group_avg[layer], mv[:, 0, 0:1],
                                                    start=True, stop=True)
                        elif kind == "gn2":
                            pe.wait_ge(gn_step, GN_STEPS * GN_STAGES.index(s) + 5)
                            last = nc.tensor.matmul(bank[:, 0:1], group_avg[layer], var_in[:, :],
                                                    start=True, stop=True)
                        elif kind in ("q", "k"):
                            if s in GN_STAGES:
                                pe.wait_ge(h_ready, GN_STAGES.index(s) + 1)
                            last = nc.tensor.matmul(bank[:, :], w_of(layer, "qk".index(kind)),
                                                    hT[:, i, cols], start=True, stop=True)
                        elif kind == "v":
                            for j in range(KT // 2):
                                t = half * KT // 2 + j
                                last = nc.tensor.matmul(bank[:, P * j:P * (j + 1)],
                                                        hT[:, i, P * t:P * (t + 1)], w_of(layer, 2),
                                                        start=True, stop=True)
                        elif kind == "shift":
                            pe.wait_ge(tile_max, TILES * (s + 1))
                            last = nc.tensor.transpose(bank[0:TILES, 0:P], neg_max[:, s % 2, :], ident)
                        elif kind == "out":
                            if s < HEAD_STAGES:
                                pe.wait_ge(o_ready, 2 * (2 * s + 1) + half + 1)
                                for g in range(2):
                                    last = nc.tensor.matmul(bank[:, :], w_out(layer, g), oT[:, g, cols],
                                                            start=g == 0, stop=g == 1)
                            else:
                                pe.wait_ge(f_out, 2 * (s - HEAD_STAGES) + half + 1)
                                last = nc.tensor.matmul(bank[:, :], w_out(layer), oT[:, 0, cols],
                                                        start=True, stop=True)
                        elif kind in ("turn", "turned"):
                            pe.wait_ge(bank_read, use["out1", s - 2 if kind == "turn" else s] + 1)
                            for j in range(KT // 2):
                                t = half * KT // 2 + j
                                last = nc.tensor.transpose(bank[:, P * j:P * (j + 1)],
                                                           xT[:, i, P * t:P * (t + 1)], ident)
                        elif kind == "back":
                            pe.wait_ge(ln_step, LN_STEPS * (LN_STAGES.index(s) + 1))
                            for j in range(KT // 2):
                                last = nc.tensor.transpose(bank[:, P * j:P * (j + 1)],
                                                           xtok[:, half * KT // 2 + j, :], ident)
                        last.then_inc(bank_full, 1)

                    def score_tile(g, n):
                        i, h, t = (g // 2) % 2, GROUP * (g % 2) + n // KT, n % KT
                        if n == 0:
                            pe.wait_ge(stacked["k"], 96 * (g // 2 + 1))
                            pe.wait_ge(stacked["q"], 96 * (g // 2 + 1))
                        if TILES * g + n >= 2:
                            pe.wait_ge(tile_max, TILES * g + n - 1)
                        for half in range(2):
                            last = nc.tensor.matmul(scores[n % 2][:, HALF * half:HALF * (half + 1)],
                                                    qs[0:STACK, i, h, P * t:P * (t + 1)],
                                                    ks[0:STACK, i, h, HALF * half:HALF * (half + 1)],
                                                    start=True, stop=True)
                        last.then_inc(tile_full, 1)

                    def turned_tile(g, slot, h):
                        t = GROUP * (SLOTS * g + slot) + h
                        i, head = (g // 2) % 2, GROUP * (g % 2) + h
                        half, key = slot // KT, slot % KT
                        if slot == 0 and h == 0:
                            pe.wait_ge(shift_in, 32 * (g + 1))
                        if t >= 2:
                            pe.wait_ge(exp_done, t - 1)
                        nc.tensor.matmul(turned[:, t % 2, :],
                                         ks[0:STACK + SHIFT, i, head, P * key:P * (key + 1)],
                                         qs[0:STACK + SHIFT, i, head, HALF * half:HALF * (half + 1)],
                                         start=True, stop=True).then_inc(turned_full, 1)

                    def values(u):
                        g, key = u // SLOTS, u % KT
                        pe.wait_ge(exp_done, GROUP * (u + 1))
                        if key == 0 and u > 0:
                            pe.wait_ge(o_copied, u // KT)
                        for h in range(GROUP):
                            last = nc.tensor.matmul(outs[2 * HD * h:2 * HD * (h + 1), :],
                                                    v_heads[:, (g // 2) % 2, key, GROUP * (g % 2) + h, :],
                                                    probs[:, u % PROB_RING, h, :],
                                                    start=key == 0, stop=key == KT - 1)
                        last.then_inc(pv_done, 1)

                    for c in FIRST:
                        chunk(*c)
                    for n in range(TILES):
                        score_tile(0, n)
                    chunk("shift", 0)
                    for g in range(N_GROUPS):
                        for slot in range(SLOTS):
                            u = SLOTS * g + slot
                            tiles = list(tiles_of_slot(g + 1, slot))
                            turned_tile(g, slot, 0)
                            for c in heads.get((g, slot), []):
                                chunk(*c)
                            turned_tile(g, slot, 1)
                            for n in tiles[0:1]:
                                score_tile(g + 1, n)
                            turned_tile(g, slot, 2)
                            if u > 0:
                                values(u - 1)
                            turned_tile(g, slot, 3)
                            for n in tiles[1:]:
                                score_tile(g + 1, n)
                    values(SLOTS * N_GROUPS - 1)

                    def full_scores(s, t):
                        n = KT * (s - HEAD_STAGES) + t
                        if n >= 2:
                            pe.wait_ge(f_exp, n - 1)
                        for half in range(2):
                            last = nc.tensor.matmul(scores[n % 2][:, HALF * half:HALF * (half + 1)],
                                                    q32[:, s % 2, P * t:P * (t + 1)],
                                                    k32[:, s % 2, HALF * half:HALF * (half + 1)],
                                                    start=True, stop=True)
                        last.then_inc(f_scores, 1)

                    def full_turn(n):
                        pe.wait_ge(f_norm, n + 1)
                        if n >= 1:
                            pe.wait_ge(f_copied_lo, n)
                            pe.wait_ge(f_copied_hi, n)
                        for k in range(KT):
                            last = nc.tensor.transpose(
                                turned[:, k // (KT // 2), P * (k % (KT // 2)):P * (k % (KT // 2) + 1)],
                                p_full[:, n % 2, P * k:P * (k + 1)], ident)
                        last.then_inc(f_turned, 1)

                    def full_values(s, half):
                        m = s - HEAD_STAGES
                        copied = KT * m + (half + 1) * KT // 2
                        pe.wait_ge(f_copied_lo, copied)
                        pe.wait_ge(f_copied_hi, copied)
                        if 2 * m + half >= 1:
                            pe.wait_ge(f_out, 2 * m + half)
                        for k in range(KT):
                            last = nc.tensor.matmul(outs[:, :], v_full[:, s % 2, k, :],
                                                    pT_full[:, k, HALF * half:HALF * (half + 1)],
                                                    start=k == 0, stop=k == KT - 1)
                        last.then_inc(f_pv, 1)

                    pe.wait_ge(tile_max, TILES * N_GROUPS)
                    pe.wait_ge(exp_done, GROUP * SLOTS * N_GROUPS)
                    pe.wait_ge(o_copied, 2 * N_GROUPS)
                    for s in range(HEAD_STAGES, STAGES):
                        pe.wait_ge(bank_read, use["v1", s] + 1)
                        full_scores(s, 0)
                        full_scores(s, 1)
                        for t in range(KT):
                            full_turn(KT * (s - HEAD_STAGES) + t)
                            if t + 2 < KT:
                                full_scores(s, t + 2)
                            for c in fulls.get((s, t), []):
                                chunk(*c)
                        for half in range(2):
                            full_values(s, half)
                    for c in LAST:
                        chunk(*c)
            nc.all_engine_barrier(sems_to_clear=range(loop_sems[0].num, loop_sems[-1].num + 1))


def kernel(**inputs):
    import numpy as np
    import concourse.bacc as _bacc
    from concourse import mybir as _mybir
    from concourse.bass_utils import run_bass_kernel_spmd as _run

    a = {n: np.asarray(v) for n, v in inputs.items()}
    C = CHANNELS

    def by_kind(w):
        return w.reshape(w.shape[0], HEADS, 3, HD).transpose(0, 2, 1, 3).reshape(w.shape[0], 3 * C)

    def padded(w):
        rows = np.zeros((HEADS, 2 * HD, C), w.dtype)
        rows[:, :HD] = w.reshape(HEADS, HD, C)
        return rows.reshape(2, P, C).transpose(1, 0, 2).reshape(P, 2 * C)

    none = np.zeros((C,), np.float32)
    b1 = by_kind(a["L1_conv_b_qkv"][None])[0]
    weights = np.concatenate([
        by_kind(a["L0_conv_w_qkv"]), by_kind(a["L1_conv_w_qkv"]),
        a["L2_conv_Wq"], a["L2_conv_Wk"], a["L2_conv_Wv"],
        a["L3_conv_wq"], a["L3_conv_wk"], a["L3_conv_wv"],
        padded(a["L0_conv_w_out"]), padded(a["L1_conv_w_out"]),
        a["L2_conv_Wp"], a["L3_conv_wp"]], axis=1)
    vectors = np.stack([
        a["L0_conv_gn_scale"], a["L0_conv_gn_bias"], none, none, a["L0_conv_b_out"],
        a["L1_conv_gn_scale"], a["L1_conv_gn_bias"], b1[:C], b1[C:2 * C], a["L1_conv_b_out"],
        a["L2_conv_ln_g"], a["L2_conv_ln_b"], a["L2_conv_bq"], a["L2_conv_bk"], a["L2_conv_bp"],
        a["L3_conv_gamma"], a["L3_conv_beta"], a["L3_conv_bq"], a["L3_conv_bk"], a["L3_conv_bp"]],
        axis=1)
    v_bias = np.stack([none, b1[2 * C:], a["L2_conv_bv"], a["L3_conv_bv"]])
    block8 = np.kron(np.eye(C // 8), np.full((8, 8), 1 / 8)).astype(np.float32)
    block4 = np.kron(np.eye(C // 4), np.full((4, 4), 1 / 4)).astype(np.float32)
    averages = np.concatenate([block8, block4, np.eye(C, dtype=np.float32),
                               np.eye(C, dtype=np.float32)], axis=1)
    arrays = {"x": a["x"].reshape(IMAGES, TOKENS, C), "weights": weights, "vectors": vectors,
              "v_bias": v_bias, "averages": averages}
    arrays = {n: np.ascontiguousarray(v) for n, v in arrays.items()}

    nc = _bacc.Bacc("TRN2", target_bir_lowering=False, num_devices=1)
    args = [nc.dram_tensor(n, v.shape, _mybir.dt.from_np(v.dtype), kind="ExternalInput").ap()
            for n, v in arrays.items()]
    out = nc.dram_tensor("out", (IMAGES, TOKENS, C), _mybir.dt.float32, kind="ExternalOutput").ap()
    attention_blocks(nc, *args, out)
    r = _run(nc, [arrays], core_ids=[0])
    return r.results[0]["out"].reshape(a["x"].shape)
```

```python
from contextlib import ExitStack

import numpy as np
import concourse.bass as bass
from concourse import mybir

P = 128
IMAGES, TOKENS, CHANNELS = 8, 1024, 128
PAIR = 2
STAGES = 8
NEXT = STAGES
HEAD_STAGES = 4
HEADS, HD = 8, 16
GROUP = 4
KT = TOKENS // P
HALF = TOKENS // 2
QT = KT // 2

ROUNDS = 4 * HEAD_STAGES
SLOTS = KT * ROUNDS
TILES = GROUP * KT
AHEAD = 3
PROB_RING = 3
WORK_BANKS = 3
HEAD_SCALE = float(HD) ** -0.5
FULL_SCALE = float(CHANNELS) ** -0.5
GN_EPS, LN_EPS = 1e-5, 1e-3

Q_PART = [0, 0, 0, 1, 1, 2]
K_PART = [0, 1, 2, 0, 1, 0]
STACK = HD * len(Q_PART)
SHIFT = 2
TWO_ONES = float(np.uint32(0x3F803F80).view(np.float32))

F32, BF16 = mybir.dt.float32, mybir.dt.bfloat16
ALU = mybir.AluOpType
ACT = mybir.ActivationFunctionType
AX_X = mybir.AxisListType.X

GN_STEPS, LN_STEPS = 8, 4
LN_STAGES = [4, 5]
NO_BANK = ("stats", "apply", "ln")


def layer_of(s):
    return s % STAGES // 2


def projections(s):
    return [(n, s) for n in ("k0", "k1", "q0", "q1", "v0", "v1")]


def head_chunks():
    at = {}

    def put(slot, *names):
        at.setdefault(slot, []).extend(names)

    put(2, ("in0", 1))
    put(3, ("in1", 1))
    for s in range(HEAD_STAGES):
        a = 4 * KT * s
        if s >= 1:
            put(a - 4, ("out0", s - 1))
            put(a + 4, ("out1", s - 1))
        if s + 1 < HEAD_STAGES:
            for i, n in enumerate(("stats", "gn1", "gn2", "apply")):
                put(a + 5 + i, (n, s + 1))
        else:
            for i, n in zip((5, 6, 7, 8, 9), ("turn0", "turn1", "ln", "back0", "back1")):
                put(a + i, (n, s + 1))
        for i, n in enumerate(projections(s + 1)):
            put(a + 9 + i, n)
    put(SLOTS - 4, ("out0", HEAD_STAGES - 1))
    for r in range(1, ROUNDS):
        put(KT * (r - 1) + (5 if r > 1 else 6), ("shift", r))
    return at


def full_chunks(then):
    at = {}

    def put(s, t, *names):
        at.setdefault((s, t), []).extend(names)

    for s in range(HEAD_STAGES, STAGES):
        if s > HEAD_STAGES:
            put(s, 0, ("out0", s - 1))
        put(s, 1 if s > HEAD_STAGES else 0, ("out1", s - 1))
        n = s + 1
        if n in LN_STAGES:
            put(s, 1, ("turn0", n), ("turn1", n))
            put(s, 2, ("ln", n))
            put(s, 3, ("back0", n), ("back1", n))
        elif n < STAGES:
            put(s, 2, ("stats", n), ("gn1", n))
            put(s, 3, ("gn2", n), ("apply", n))
        if n < STAGES:
            for i, c in enumerate(projections(n)):
                put(s, 4 + i // 2, c)
    if then:
        put(STAGES - 2, 6, ("in0", NEXT))
        put(STAGES - 2, 7, ("in1", NEXT))
        put(STAGES - 1, 0, ("stats", NEXT), ("gn1", NEXT))
        put(STAGES - 1, 1, ("gn2", NEXT), ("apply", NEXT))
        for i, c in enumerate(projections(NEXT)):
            put(STAGES - 1, 2 + i // 2, c)
    put(STAGES - 1, 5, ("turned0", STAGES - 2))
    put(STAGES - 1, 6, ("turned1", STAGES - 2))
    return at


def tile_slots():
    at = {}
    for r in range(1, ROUNDS):
        for n in range(TILES):
            slot = KT * (r - 1) - AHEAD + n // GROUP if r > 1 else 6 * n // TILES
            at.setdefault(slot, []).append((r, n))
    return at


class Plan:

    FIRST = [("in0", NEXT), ("in1", NEXT), ("stats", NEXT), ("gn1", NEXT), ("gn2", NEXT),
             ("apply", NEXT), *projections(NEXT)]

    def __init__(self, main, then):
        self.main, self.then = main, then
        self.heads, self.fulls, self.tiles = head_chunks(), full_chunks(then), tile_slots()
        self.order = []
        if main:
            for slot in range(SLOTS):
                self.order += self.slot(slot)
            for s in range(HEAD_STAGES, STAGES):
                for t in range(KT):
                    self.order.append(("turn", KT * (s - HEAD_STAGES) + t))
                    self.order += [("chunk", c) for c in self.fulls.get((s, t), [])]
            self.order += self.tail()
        else:
            self.order += [("chunk", c) for c in self.FIRST]
            self.order += [("tile", (ROUNDS, n)) for n in range(TILES)]
            self.order.append(("chunk", ("shift", ROUNDS)))
        self.stages = (list(range(1, STAGES)) if main else []) + [NEXT] * then
        self.gn_stages = [s for s in self.stages if s not in LN_STAGES]
        self.head_stages = [s for s in self.stages if s < HEAD_STAGES or s == NEXT]
        self.rounds = (list(range(1, ROUNDS)) if main else []) + [ROUNDS] * then
        self.bank, self.before, self.use, held, turn = {}, {}, {}, {}, 0
        for item in self.order:
            kind, key = item
            if kind == "chunk" and key[0] in NO_BANK or kind in ("pair", "values"):
                continue
            if kind == "turn":
                banks = [0, 1]
            elif not main or self.in_rounds(item):
                banks = [turn % WORK_BANKS]
                turn += 1
            elif kind == "tile":
                banks = [key[1] % 2]
            else:
                banks = [2]
            self.bank[item] = banks[0]
            self.before[item] = [held[b] for b in banks if b in held]
            for b in banks:
                held[b] = item
            if kind == "chunk":
                self.use[key] = len(self.use)

    def in_rounds(self, item):
        kind, key = item
        if kind == "tile":
            return key[0] < ROUNDS
        return any(key in c for c in self.heads.values())

    def slot(self, slot):
        tiles = [("tile", t) for t in self.tiles.get(slot, [])]
        chunks = [("chunk", c) for c in self.heads.get(slot, [])]
        return [("pair", 2 * slot), *tiles[0:2], ("pair", 2 * slot + 1), *tiles[2:3],
                ("values", slot - 1), *tiles[3:], *chunks]

    def tail(self):
        chunks = [("chunk", (n, STAGES - 1)) for n in ("out0", "out1", "turned0", "turned1")]
        tiles = [("tile", (ROUNDS, n)) for n in range(TILES)] if self.then else []
        order = []
        for half in range(2):
            for k in range(KT):
                order += [("values", ("last", half, k)), *tiles[:1]]
                tiles = tiles[1:]
            if half == 1:
                order.append(chunks[0])
        for c in chunks[1:]:
            order += [*tiles[:5], c]
            tiles = tiles[5:]
        order += tiles
        if self.then:
            order.append(("chunk", ("shift", ROUNDS)))
        return order

    def tile_ordinal(self, r, n):
        return TILES * self.rounds.index(r) + n


def attention_blocks(nc, x, weights, vectors, v_bias, averages, out):
    with ExitStack() as ctx:
        def sb(name, shape, dt=F32):
            return ctx.enter_context(nc.sbuf_tensor(name, shape, dt))

        def psum(name, shape, dt=F32):
            return ctx.enter_context(nc.psum_tensor(name, shape, dt))

        loop_sems = []

        def sem(name):
            s = ctx.enter_context(nc.semaphore(name))
            loop_sems.append(s)
            return s

        w = sb("w", [P, weights.shape[1]])
        vec = sb("vec", [P, vectors.shape[1]])
        qbias = sb("qbias", [P, 4])
        vb = sb("vb", [P, 4, CHANNELS])
        avg = sb("avg", [P, 3 * P])
        minus_half = sb("minus_half", [P, KT])
        xin = sb("xin", [P, PAIR, KT, CHANNELS])
        x_next = sb("x_next", [P, TOKENS])
        xT = sb("xT", [P, PAIR, TOKENS])
        hT = sb("hT", [P, PAIR, TOKENS])
        xtok = sb("xtok", [P, KT, CHANNELS])
        q32 = sb("q32", [P, PAIR, TOKENS])
        k32 = sb("k32", [P, PAIR, TOKENS])
        q_parts = sb("q_parts", [P, 3, 2, HALF], BF16)
        k_parts = sb("k_parts", [P, 3, 2, HALF], BF16)
        rest = sb("rest", [P, HALF])
        q_stack = sb("q_stack", [P, PAIR * HEADS * TOKENS], BF16)
        k_stack = sb("k_stack", [P, PAIR * HEADS * TOKENS], BF16)
        v_heads = sb("v_heads", [P, PAIR, KT, HEADS, 2 * HD])
        v_full = sb("v_full", [P, PAIR, KT, CHANNELS])
        probs = sb("probs", [P, PROB_RING, GROUP, HALF])
        o_turn = sb("o_turn", [P, 2, HALF // 32, 32])
        o_scale = sb("o_scale", [P, 2, HALF // 32, 32])
        o_inv = sb("o_inv", [P, 2, HALF // 32])
        oT = sb("oT", [P, 2, TOKENS])
        part_max = sb("part_max", [P, 2, TILES])
        neg_max = sb("neg_max", [P, 2, TILES // 2])
        shift_parts = sb("shift_parts", [TILES // 2, 2, P], BF16)
        stats = sb("stats", [P, KT, nc.vector.BN_STATS_DIM])
        mv = sb("mv", [P, KT, 2])
        gmean = sb("gmean", [P, 1])
        dev = sb("dev", [P, 1])
        var_in = sb("var_in", [P, 1])
        var_eps = sb("var_eps", [P, KT])
        rstd = sb("rstd", [P, KT])
        gscale = sb("gscale", [P, 1])
        gshift = sb("gshift", [P, 2])
        neg_max1 = sb("neg_max1", [P, 4])
        sum1 = sb("sum1", [P, 4])
        inv1 = sb("inv1", [P, 4])

        qs = q_stack[:, :].rearrange("p (i a h t) -> p i a h t", i=PAIR, a=2, h=HEADS)
        ks = k_stack[:, :].rearrange("p (i a h t) -> p i a h t", i=PAIR, a=2, h=HEADS)
        p_full = probs[:, 0, :, :].rearrange("p (n a) k -> p n (a k)", n=2)
        pT_full = [q_stack[:, HEADS * TOKENS:].bitcast(F32).rearrange("p (k q) -> p k q", k=QT),
                   probs[:, 1:3, :, :].rearrange("p n (m a) k -> p (n m) (a k)", m=2)]

        ident = avg[:, 2 * P:3 * P]
        group_avg = {0: avg[:, 0:P], 1: avg[:, P:2 * P], 3: avg[:, P:2 * P]}

        def w_of(layer, n):
            return w[:, (3 * layer + n) * P:(3 * layer + n + 1) * P]

        def w_out(layer, g=0):
            n = 12 + (2 * layer + g if layer < 2 else 2 + layer)
            return w[:, n * P:(n + 1) * P]

        def vec_of(layer, n):
            return vec[:, 5 * layer + n:5 * layer + n + 1]

        pairs = psum("pairs", [P, 2, 2, HALF])
        outs = psum("outs", [P, HALF])
        work = psum("work", [P, WORK_BANKS, HALF])

        scratch = {n: nc.dram_tensor(f"{n}_scratch", [3, 2 * HEADS, HD, HALF], BF16, kind="Internal").ap()
                   for n in "qk"}

        setup_loads = sem("setup_loads")
        qbias_ready = sem("qbias_ready")
        image_loaded = sem("image_loaded")
        bank_full = sem("bank_full")
        bank_read = sem("bank_read")
        gn_step = sem("gn_step")
        ln_step = sem("ln_step")
        rstd_ready = sem("rstd_ready")
        h_ready = sem("h_ready")
        split = sem("split")
        parts_out = {n: sem(f"{n}_parts_out") for n in "qk"}
        stacked = {n: sem(f"{n}_stacked") for n in "qk"}
        tile_full = sem("tile_full")
        tile_max = sem("tile_max")
        max_ready = sem("max_ready")
        shift_hi = sem("shift_hi")
        shift_in = sem("shift_in")
        pair_full = sem("pair_full")
        exp_done = sem("exp_done")
        pv_done = sem("pv_done")
        o_turned = sem("o_turned")
        o_inverse = sem("o_inverse")
        o_scaled = sem("o_scaled")
        o_ready = sem("o_ready")
        f_scores = sem("f_scores")
        f_max = sem("f_max")
        f_exp = sem("f_exp")
        f_inv = sem("f_inv")
        f_norm = sem("f_norm")
        f_turned = sem("f_turned")
        f_copied = [sem("f_copied_lo"), sem("f_copied_hi")]
        f_pv = sem("f_pv")
        f_out = sem("f_out")
        y_stored = sem("y_stored")

        def run(plan, loads, stores):
            use = plan.use
            main, then = plan.main, plan.then

            def half_of(name):
                return int(name[-1]) if name[-1] in "01" else 0

            def kind_of(name):
                return name if name in ("gn1", "gn2") else name.rstrip("01")

            def x_of(s):
                return x_next[:, :] if s == NEXT else xT[:, s % 2, :]

            def tiles_of(half):
                return slice(QT * half, QT * (half + 1))

            def result_of(s):
                return xtok[:, :, :] if s % 2 == 0 else hT[:, 1, :].rearrange("p (j c) -> p j c", j=KT)

            def bank_of(name, s):
                return work[:, plan.bank["chunk", (name, s)], :]

            with nc.Block() as block:
                @block.sync
                def _(sp):
                    def load_images():
                        for i, image in enumerate(loads):
                            sp.dma_start(xin[:, i, :, :], image).then_inc(image_loaded, 16)

                    def stack(s):
                        n_th = plan.head_stages.index(s)
                        for i, (n, parts) in enumerate((("k", k_parts), ("q", q_parts))):
                            sp.wait_ge(split, 12 * n_th + 6 * (i + 1))
                            for j in range(3):
                                to = scratch[n][j].rearrange("(a h) r t -> (h r) a t", a=2)
                                sp.dma_start(to, parts[:, j, :, :]).then_inc(parts_out[n], 16)
                        for n, to, which in (("k", ks, K_PART), ("q", qs, Q_PART)):
                            sp.wait_ge(parts_out[n], 48 * (n_th + 1))
                            for j, part in enumerate(which):
                                rows = to[HD * j:HD * (j + 1), s % 2, :, :, :]
                                sp.dma_start(rows.rearrange("r a h t -> r (a h) t"),
                                             scratch[n][part].rearrange("m r t -> r m t")
                                             ).then_inc(stacked[n], 16)

                    def shift(r):
                        first = GROUP * (r // 2 % 2)
                        sp.wait_ge(bank_read, use["shift", r] + 1)
                        for j in range(SHIFT):
                            row = qs[STACK + j:STACK + j + 1, r // 4 % 2, r % 2, first:first + GROUP, :]
                            sp.dma_start(row.rearrange("o h (n q) -> o (h n) q", n=QT),
                                         shift_parts[:, j, :]).then_inc(shift_in, 16)

                    def store(i, image):
                        sp.wait_ge(bank_read, use["turned1", STAGES - PAIR + i] + 1)
                        sp.dma_start(image, result_of(i)).then_inc(y_stored, 16)

                    if not main:
                        load_images()
                        sp.dma_start(avg[:, :], averages).then_inc(setup_loads, 16)
                        sp.dma_start(vec[:, :], vectors).then_inc(setup_loads, 16)
                        sp.dma_start(w[:, :], weights).then_inc(setup_loads, 16)
                        sp.dma_start(vb[:, :, :], v_bias.partition_broadcast(P)).then_inc(setup_loads, 16)
                        stack(NEXT)
                        shift(ROUNDS)
                        sp.wait_ge(shift_in, 32 * len(plan.rounds))
                        return
                    if then:
                        sp.wait_ge(bank_read, use["in1", 1] + 1)
                        load_images()
                    for r in range(1, ROUNDS):
                        if r % 4 == 3 and r // 4 + 1 < HEAD_STAGES:
                            stack(r // 4 + 1)
                        shift(r)
                    if then:
                        stack(NEXT)
                    for i, image in enumerate(stores):
                        store(i, image)
                    if then:
                        shift(ROUNDS)
                        sp.wait_ge(shift_in, 32 * len(plan.rounds))
                    sp.wait_ge(y_stored, 16 * PAIR)

                @block.gpsimd
                def _(pool):
                    def inverse_root(s):
                        n = KT if s in LN_STAGES else 1
                        if s in LN_STAGES:
                            pool.wait_ge(ln_step, LN_STEPS * LN_STAGES.index(s) + 3)
                        else:
                            pool.wait_ge(bank_read, use["gn2", s] + 1)
                        nc.gpsimd.tensor_tensor(rstd[:, 0:n], var_eps[:, 0:n], minus_half[:, 0:n],
                                                ALU.pow).then_inc(rstd_ready, 1)

                    def split_half(s, name):
                        whole, parts = (k32, k_parts) if name[0] == "k" else (q32, q_parts)
                        t = half_of(name)
                        done = 12 * plan.head_stages.index(s) + 3 * ["k0", "k1", "q0", "q1"].index(name)
                        pool.wait_ge(bank_read, use[name, s] + 1)
                        if done:
                            pool.wait_ge(split, done)
                        nc.gpsimd.tensor_tensor(rest[:, :], whole[:, s % 2, HALF * t:HALF * (t + 1)],
                                                parts[:, 0, t, :], ALU.subtract).then_inc(split, 1)
                        pool.wait_ge(split, done + 1)
                        nc.gpsimd.tensor_copy(parts[:, 1, t, :], rest[:, :]).then_inc(split, 1)
                        pool.wait_ge(split, done + 2)
                        nc.gpsimd.tensor_tensor(parts[:, 2, t, :], rest[:, :], parts[:, 1, t, :],
                                                ALU.subtract).then_inc(split, 1)

                    def scale_outputs(r):
                        pool.wait_ge(o_inverse, r + 1)
                        if r >= 2:
                            pool.wait_ge(o_ready, r - 1)
                        inv = o_inv[:, r % 2, :].unsqueeze(2).to_broadcast([P, HALF // 32, 32])
                        nc.gpsimd.tensor_tensor(o_scale[:, r % 2, :, :], o_turn[:, r % 2, :, :], inv,
                                                ALU.mult).then_inc(o_scaled, 1)

                    if not main:
                        inverse_root(NEXT)
                        for n, _ in projections(NEXT)[:4]:
                            split_half(NEXT, n)
                        return
                    for s in range(HEAD_STAGES):
                        if s >= 1:
                            scale_outputs(4 * s - 1)
                        inverse_root(s + 1)
                        for n, _ in projections(s + 1)[:4] if s + 1 < HEAD_STAGES else ():
                            split_half(s + 1, n)
                            if n == "k0":
                                scale_outputs(4 * s)
                        if s + 1 == HEAD_STAGES:
                            scale_outputs(4 * s)
                        scale_outputs(4 * s + 1)
                        scale_outputs(4 * s + 2)
                    scale_outputs(ROUNDS - 1)
                    for s in range(HEAD_STAGES + 1, STAGES):
                        inverse_root(s)
                    if then:
                        inverse_root(NEXT)
                        for n, _ in projections(NEXT)[:4]:
                            split_half(NEXT, n)

                @block.scalar
                def _(act):
                    def chunk(name, s):
                        kind, half, layer = kind_of(name), half_of(name), layer_of(s)
                        if kind not in ("in", "turn", "back", "q", "k", "shift", "turned"):
                            return
                        cols = slice(HALF * half, HALF * (half + 1))
                        bank = bank_of(name, s)
                        by_token = bank.rearrange("p (j c) -> p j c", c=CHANNELS)
                        if kind == "shift" and s > plan.rounds[0]:
                            act.wait_ge(shift_in, 32 * plan.rounds.index(s))
                        act.wait_ge(bank_full, use[name, s] + 1)
                        if kind == "in":
                            nc.scalar.copy(x_of(s)[:, cols], bank).then_inc(bank_read, 1)
                        elif kind == "turn":
                            nc.scalar.copy(xtok[:, tiles_of(half), :], by_token).then_inc(bank_read, 1)
                        elif kind == "back":
                            nc.scalar.activation(hT[:, s % 2, cols], bank, ACT.Identity,
                                                 bias=vec_of(layer, 1), scale=vec_of(layer, 0)
                                                 ).then_inc(bank_read, 1)
                        elif kind in ("q", "k"):
                            to, parts, bias, scale = (k32, k_parts, vec_of(layer, 3), 1.0)
                            if kind == "q":
                                to, parts, bias = q32, q_parts, qbias[:, layer:layer + 1]
                                scale = 1.0 if layer < 2 else FULL_SCALE
                            last = nc.scalar.activation(to[:, s % 2, cols], bank, ACT.Identity,
                                                        bias=bias, scale=scale)
                            if s in plan.head_stages:
                                last = nc.scalar.activation(parts[:, 0, half, :], bank, ACT.Identity,
                                                            bias=bias, scale=scale)
                            last.then_inc(bank_read, 1)
                        elif kind == "shift":
                            nc.scalar.copy(shift_parts[:, 0, :], bank[0:TILES // 2, 0:P]
                                           ).then_inc(shift_hi, 1)
                        elif kind == "turned":
                            nc.scalar.copy(result_of(s)[:, tiles_of(half), :], by_token
                                           ).then_inc(bank_read, 1)

                    def exp(u, n):
                        t = 2 * u + n
                        if n == 0 and u >= PROB_RING:
                            act.wait_ge(pv_done, u - PROB_RING + 1)
                        act.wait_ge(pair_full, t + 1)
                        nc.scalar.activation(probs[:, u % PROB_RING, 2 * n:2 * n + 2, :],
                                             pairs[:, t % 2, :, :], ACT.Exp, scale=HEAD_SCALE
                                             ).then_inc(exp_done, 1)

                    def full_exp(n):
                        act.wait_ge(f_max, n + 1)
                        if n >= 2:
                            act.wait_ge(f_turned, n - 1)
                        nc.scalar.activation(p_full[:, n % 2, :],
                                             pairs[:, n % 2, :, :].rearrange("p a k -> p (a k)"), ACT.Exp,
                                             bias=neg_max1[:, n % 4:n % 4 + 1],
                                             accum_out=sum1[:, n % 4:n % 4 + 1]).then_inc(f_exp, 1)

                    def full_out(m, half):
                        act.wait_ge(f_pv, 2 * m + half + 1)
                        nc.scalar.copy(oT[:, 0, HALF * half:HALF * (half + 1)], outs[:, :]
                                       ).then_inc(f_out, 1)

                    if not main:
                        act.wait_ge(qbias_ready, 4)
                        for kind, key in plan.order:
                            if kind == "chunk":
                                chunk(*key)
                        return
                    for slot in range(SLOTS):
                        exp(slot, 0)
                        exp(slot, 1)
                        for c in plan.heads.get(slot, []):
                            chunk(*c)
                    full_exp(0)
                    full_exp(1)
                    for m, s in enumerate(range(HEAD_STAGES, STAGES)):
                        for t in range(KT):
                            n = KT * m + t
                            if t == 6 and s + 1 < STAGES:
                                full_out(m, 0)
                            act.wait_ge(f_turned, n + 1)
                            if t == 0 and m >= 1:
                                act.wait_ge(f_pv, 2 * m)
                            nc.scalar.copy(pT_full[0][:, :, P * t:P * (t + 1)],
                                           work[:, 0, :].rearrange("p (k q) -> p k q", q=P)
                                           ).then_inc(f_copied[0], 1)
                            if t + 2 < KT:
                                full_exp(n + 2)
                            for c in plan.fulls.get((s, t), []):
                                chunk(*c)
                        if s + 1 < STAGES:
                            full_exp(KT * (m + 1))
                            full_out(m, 1)
                            full_exp(KT * (m + 1) + 1)
                    for kind, key in plan.tail():
                        if kind == "chunk":
                            chunk(*key)
                        elif kind == "values" and key[2] == KT - 1:
                            full_out(STAGES - 1 - HEAD_STAGES, key[1])

                @block.vector
                def _(dve):
                    def chunk(name, s):
                        kind, half, layer = kind_of(name), half_of(name), layer_of(s)
                        cols = slice(HALF * half, HALF * (half + 1))
                        if s in plan.gn_stages:
                            step0 = GN_STEPS * plan.gn_stages.index(s)
                        if kind == "stats":
                            source = ("in1", s) if s in (1, NEXT) else ("out1", s - 2)
                            dve.wait_ge(bank_read, use[source] + 1)
                            for t in range(2):
                                nc.vector.bn_stats(stats[:, t, :], x_of(s)[:, HALF * t:HALF * (t + 1)]
                                                   ).then_inc(gn_step, 1)
                            dve.wait_ge(gn_step, step0 + 2)
                            nc.vector.bn_aggr(mv[:, 0, :], stats[:, 0:2, :]).then_inc(gn_step, 1)
                        elif kind == "gn1":
                            dve.wait_ge(bank_full, use[name, s] + 1)
                            nc.vector.tensor_copy(gmean[:, :], bank_of(name, s)[:, 0:1]
                                                  ).then_inc(bank_read, 1)
                            dve.wait_ge(bank_read, use[name, s] + 1)
                            nc.vector.tensor_tensor(dev[:, :], mv[:, 0, 0:1], gmean[:, :], ALU.subtract
                                                    ).then_inc(gn_step, 1)
                            dve.wait_ge(gn_step, step0 + 4)
                            nc.vector.scalar_tensor_tensor(var_in[:, :], dev[:, :], dev[:, :],
                                                           mv[:, 0, 1:2], ALU.mult, ALU.add
                                                           ).then_inc(gn_step, 1)
                        elif kind == "gn2":
                            dve.wait_ge(bank_full, use[name, s] + 1)
                            nc.vector.tensor_scalar(var_eps[:, 0:1], bank_of(name, s)[:, 0:1], GN_EPS,
                                                    None, ALU.add).then_inc(bank_read, 1)
                        elif kind == "apply":
                            dve.wait_ge(rstd_ready, plan.stages.index(s) + 1)
                            nc.vector.tensor_tensor(gscale[:, :], rstd[:, 0:1], vec_of(layer, 0),
                                                    ALU.mult).then_inc(gn_step, 1)
                            dve.wait_ge(gn_step, step0 + 6)
                            nc.vector.tensor_tensor(gshift[:, 0:1], gmean[:, :], gscale[:, :], ALU.mult
                                                    ).then_inc(gn_step, 1)
                            dve.wait_ge(gn_step, step0 + 7)
                            nc.vector.tensor_tensor(gshift[:, 1:2], vec_of(layer, 1), gshift[:, 0:1],
                                                    ALU.subtract).then_inc(gn_step, 1)
                            dve.wait_ge(gn_step, step0 + 8)
                            nc.vector.tensor_scalar(hT[:, s % 2, :], x_of(s), gscale[:, :],
                                                    gshift[:, 1:2], ALU.mult, ALU.add
                                                    ).then_inc(h_ready, 1)
                        elif kind == "ln":
                            step0 = LN_STEPS * LN_STAGES.index(s)
                            dve.wait_ge(bank_read, use["turn1", s] + 1)
                            for j in range(KT):
                                last = nc.vector.bn_stats(stats[:, j, :], xtok[:, j, :])
                            last.then_inc(ln_step, 1)
                            dve.wait_ge(ln_step, step0 + 1)
                            for j in range(KT):
                                last = nc.vector.bn_aggr(mv[:, j, :], stats[:, j, :])
                            last.then_inc(ln_step, 1)
                            dve.wait_ge(ln_step, step0 + 2)
                            nc.vector.tensor_scalar(var_eps[:, :], mv[:, :, 1], LN_EPS, None, ALU.add
                                                    ).then_inc(ln_step, 1)
                            dve.wait_ge(rstd_ready, plan.stages.index(s) + 1)
                            for j in range(KT):
                                last = nc.vector.tensor_scalar(xtok[:, j, :], xtok[:, j, :],
                                                               mv[:, j, 0:1], rstd[:, j:j + 1],
                                                               ALU.subtract, ALU.mult)
                            last.then_inc(ln_step, 1)
                        elif kind == "v":
                            dve.wait_ge(bank_full, use[name, s] + 1)
                            bank = bank_of(name, s)
                            if s in plan.head_stages:
                                bias = vb[:, layer, :].rearrange("p (h d) -> p h d", h=HEADS)
                                for j in range(QT):
                                    last = nc.vector.tensor_tensor(
                                        v_heads[:, s % 2, QT * half + j, :, 0:HD],
                                        bank[:, P * j:P * (j + 1)].rearrange("p (h d) -> p h d", h=HEADS),
                                        bias, ALU.add)
                            else:
                                bias = vb[:, layer, :].unsqueeze(1).to_broadcast([P, QT, CHANNELS])
                                last = nc.vector.tensor_tensor(
                                    v_full[:, s % 2, tiles_of(half), :],
                                    bank.rearrange("p (j c) -> p j c", c=CHANNELS), bias, ALU.add)
                            last.then_inc(bank_read, 1)
                        elif kind == "shift":
                            dve.wait_ge(shift_hi, plan.rounds.index(s) + 1)
                            nc.vector.tensor_tensor(shift_parts[:, 1, :],
                                                    bank_of(name, s)[0:TILES // 2, 0:P],
                                                    shift_parts[:, 0, :], ALU.subtract
                                                    ).then_inc(bank_read, 1)
                        elif kind == "out":
                            skip = hT[:, s % 2, :] if layer == 1 else x_of(s)
                            if s == 0:
                                skip = x_next[:, :]
                            dve.wait_ge(bank_full, use[name, s] + 1)
                            nc.vector.scalar_tensor_tensor(xT[:, s % 2, cols], bank_of(name, s),
                                                           vec_of(layer, 4), skip[:, cols], ALU.add,
                                                           ALU.add).then_inc(bank_read, 1)

                    def tile_maximum(r, n):
                        t = plan.tile_ordinal(r, n)
                        dve.wait_ge(tile_full, t + 1)
                        nc.vector.tensor_reduce(part_max[:, r % 2, n:n + 1],
                                                work[:, plan.bank["tile", (r, n)], :], AX_X, ALU.max,
                                                negate=True).then_inc(tile_max, 1)
                        if n == TILES - 1:
                            dve.wait_ge(tile_max, t + 1)
                            nc.vector.tensor_reduce(neg_max[:, r % 2, :],
                                                    part_max[:, r % 2, :].rearrange(
                                                        "p (n a) -> p n a", a=2), AX_X, ALU.min
                                                    ).then_inc(max_ready, 1)

                    def turn_outputs(r):
                        dve.wait_ge(pv_done, KT * (r + 1))
                        if r >= 2:
                            dve.wait_ge(o_scaled, r - 1)
                        nc.vector.transpose(o_turn[:, r % 2, :, :].rearrange("p b c -> p (b c)"),
                                            outs[:, :]).then_inc(o_turned, 1)
                        dve.wait_ge(o_turned, r + 1)
                        nc.vector.reciprocal(o_inv[:, r % 2, :], o_turn[:, r % 2, :, HD]
                                             ).then_inc(o_inverse, 1)

                    def turn_back(r):
                        half = slice(HALF * (r % 2), HALF * (r % 2 + 1))
                        dve.wait_ge(o_scaled, r + 1)
                        nc.vector.transpose(oT[:, r // 2 % 2, half],
                                            o_scale[:, r % 2, :, :].rearrange("p b c -> p (b c)")
                                            ).then_inc(o_ready, 1)

                    def full_max(n):
                        dve.wait_ge(f_scores, n + 1)
                        nc.vector.tensor_reduce(neg_max1[:, n % 4:n % 4 + 1],
                                                pairs[:, n % 2, :, :].rearrange("p a k -> p (a k)"),
                                                AX_X, ALU.max, negate=True).then_inc(f_max, 1)

                    if not main:
                        nc.vector.memset(minus_half[:, :], -0.5)
                        nc.vector.memset(v_heads[:, :, :, :, HD:2 * HD], 1.0)
                        nc.vector.memset(k_stack[STACK:STACK + SHIFT, :].bitcast(F32), TWO_ONES)
                        dve.wait_ge(setup_loads, 64)
                        for layer in range(4):
                            scale = 1.0 if layer < 2 else FULL_SCALE
                            nc.vector.tensor_scalar(qbias[:, layer:layer + 1], vec_of(layer, 2), scale,
                                                    None, ALU.mult).then_inc(qbias_ready, 1)
                        for kind, key in plan.order:
                            if kind == "chunk":
                                chunk(*key)
                            elif kind == "tile":
                                tile_maximum(*key)
                        return
                    for slot in range(SLOTS):
                        r = slot // KT - 1
                        if r >= 0 and slot % KT == 1:
                            turn_outputs(r)
                        if r >= 0 and slot % KT == (7 if r % 4 < 2 else 3):
                            turn_back(r)
                        for t in plan.tiles.get(slot, []):
                            tile_maximum(*t)
                        for c in plan.heads.get(slot, []):
                            chunk(*c)
                    turn_outputs(ROUNDS - 1)
                    full_max(0)
                    turn_back(ROUNDS - 1)
                    full_max(1)
                    for m, s in enumerate(range(HEAD_STAGES, STAGES)):
                        for t in range(KT):
                            n = KT * m + t
                            dve.wait_ge(f_exp, n + 1)
                            nc.vector.reciprocal(inv1[:, n % 4:n % 4 + 1], sum1[:, n % 4:n % 4 + 1]
                                                 ).then_inc(f_inv, 1)
                            dve.wait_ge(f_inv, n + 1)
                            nc.vector.tensor_scalar(p_full[:, n % 2, :], p_full[:, n % 2, :],
                                                    inv1[:, n % 4:n % 4 + 1], None, ALU.mult
                                                    ).then_inc(f_norm, 1)
                            if t + 2 < KT:
                                full_max(n + 2)
                            dve.wait_ge(f_turned, n + 1)
                            if t == 0 and m >= 1:
                                dve.wait_ge(f_pv, 2 * m)
                            nc.vector.tensor_copy(pT_full[1][:, :, P * t:P * (t + 1)],
                                                  work[:, 1, :].rearrange("p (k q) -> p k q", q=P)
                                                  ).then_inc(f_copied[1], 1)
                            for c in plan.fulls.get((s, t), []):
                                chunk(*c)
                        if s + 1 < STAGES:
                            full_max(KT * (m + 1))
                            full_max(KT * (m + 1) + 1)
                    for kind, key in plan.tail():
                        if kind == "chunk":
                            chunk(*key)
                        elif kind == "tile":
                            tile_maximum(*key)

                @block.tensor
                def _(pe):
                    def wait_for_bank(item):
                        for kind, key in plan.before[item]:
                            if kind == "tile":
                                pe.wait_ge(tile_max, plan.tile_ordinal(*key) + 1)
                            elif kind == "turn":
                                pe.wait_ge(f_copied[0], key + 1)
                                pe.wait_ge(f_copied[1], key + 1)
                            elif item[0] != "chunk":
                                pe.wait_ge(bank_read, use[key] + 1)

                    def chunk(name, s):
                        kind, half, layer = kind_of(name), half_of(name), layer_of(s)
                        if kind in NO_BANK:
                            return
                        cols = slice(HALF * half, HALF * (half + 1))
                        bank = bank_of(name, s)
                        wait_for_bank(("chunk", (name, s)))
                        if use[name, s] >= 1:
                            pe.wait_ge(bank_read, use[name, s])
                        if kind == "in":
                            if s == NEXT:
                                pe.wait_ge(image_loaded, 16 * PAIR)
                            for j in range(QT):
                                last = nc.tensor.transpose(bank[:, P * j:P * (j + 1)],
                                                           xin[:, s % 2, QT * half + j, :], ident)
                        elif kind == "gn1":
                            pe.wait_ge(gn_step, GN_STEPS * plan.gn_stages.index(s) + 3)
                            last = nc.tensor.matmul(bank[:, 0:1], group_avg[layer], mv[:, 0, 0:1],
                                                    start=True, stop=True)
                        elif kind == "gn2":
                            pe.wait_ge(gn_step, GN_STEPS * plan.gn_stages.index(s) + 5)
                            last = nc.tensor.matmul(bank[:, 0:1], group_avg[layer], var_in[:, :],
                                                    start=True, stop=True)
                        elif kind in ("q", "k"):
                            if s in plan.gn_stages:
                                pe.wait_ge(h_ready, plan.gn_stages.index(s) + 1)
                            last = nc.tensor.matmul(bank, w_of(layer, "qk".index(kind)),
                                                    hT[:, s % 2, cols], start=True, stop=True)
                        elif kind == "v":
                            for j in range(QT):
                                t = QT * half + j
                                last = nc.tensor.matmul(bank[:, P * j:P * (j + 1)],
                                                        hT[:, s % 2, P * t:P * (t + 1)], w_of(layer, 2),
                                                        start=True, stop=True)
                        elif kind == "shift":
                            pe.wait_ge(max_ready, plan.rounds.index(s) + 1)
                            last = nc.tensor.transpose(bank[0:TILES // 2, 0:P], neg_max[:, s % 2, :],
                                                       ident)
                        elif kind == "out":
                            if s < HEAD_STAGES:
                                pe.wait_ge(o_ready, 4 * s + 2 + half + 1)
                                for g in range(2):
                                    last = nc.tensor.matmul(bank, w_out(layer, g), oT[:, g, cols],
                                                            start=g == 0, stop=g == 1)
                            else:
                                pe.wait_ge(f_out, 2 * (s - HEAD_STAGES) + half + 1)
                                last = nc.tensor.matmul(bank, w_out(layer), oT[:, 0, cols],
                                                        start=True, stop=True)
                        elif kind in ("turn", "turned"):
                            pe.wait_ge(bank_read, use["out1", s - 2 if kind == "turn" else s] + 1)
                            for j in range(QT):
                                t = QT * half + j
                                last = nc.tensor.transpose(bank[:, P * j:P * (j + 1)],
                                                           xT[:, s % 2, P * t:P * (t + 1)], ident)
                        elif kind == "back":
                            pe.wait_ge(ln_step, LN_STEPS * (LN_STAGES.index(s) + 1))
                            for j in range(QT):
                                last = nc.tensor.transpose(bank[:, P * j:P * (j + 1)],
                                                           xtok[:, QT * half + j, :], ident)
                        last.then_inc(bank_full, 1)

                    def score_tile(r, n):
                        i, head = r // 4 % 2, GROUP * (r // 2 % 2) + n // KT
                        t, keys = n // 2 % QT, n % 2
                        if n == 0 and r % 4 == 0:
                            stage = r // 4 if r < ROUNDS else NEXT
                            for name in "kq":
                                pe.wait_ge(stacked[name], 96 * (plan.head_stages.index(stage) + 1))
                        wait_for_bank(("tile", (r, n)))
                        nc.tensor.matmul(work[:, plan.bank["tile", (r, n)], :],
                                         qs[0:STACK, i, r % 2, head, P * t:P * (t + 1)],
                                         ks[0:STACK, i, keys, head, :],
                                         start=True, stop=True).then_inc(tile_full, 1)

                    def pair(u, n):
                        t, r, key = 2 * u + n, u // KT, u % KT
                        if key == 0 and n == 0 and r >= 1:
                            pe.wait_ge(shift_in, 32 * r)
                        if t >= 2:
                            pe.wait_ge(exp_done, t - 1)
                        for h in range(2):
                            head = GROUP * (r // 2 % 2) + 2 * n + h
                            last = nc.tensor.matmul(
                                pairs[:, t % 2, h, :],
                                ks[0:STACK + SHIFT, r // 4 % 2, key // QT, head,
                                   P * (key % QT):P * (key % QT + 1)],
                                qs[0:STACK + SHIFT, r // 4 % 2, r % 2, head, :], start=True, stop=True)
                        last.then_inc(pair_full, 1)

                    def values(u):
                        r, key = u // KT, u % KT
                        pe.wait_ge(exp_done, 2 * (u + 1))
                        if key == 0 and r > 0:
                            pe.wait_ge(o_turned, r)
                        for h in range(GROUP):
                            last = nc.tensor.matmul(outs[2 * HD * h:2 * HD * (h + 1), :],
                                                    v_heads[:, r // 4 % 2, key,
                                                            GROUP * (r // 2 % 2) + h, :],
                                                    probs[:, u % PROB_RING, h, :],
                                                    start=key == 0, stop=key == KT - 1)
                        last.then_inc(pv_done, 1)

                    def full_scores(s, t):
                        n = KT * (s - HEAD_STAGES) + t
                        if t == 0:
                            pe.wait_ge(bank_read, use["q1", s] + 1)
                        if n >= 2:
                            pe.wait_ge(f_exp, n - 1)
                        for half in range(2):
                            last = nc.tensor.matmul(pairs[:, n % 2, half, :],
                                                    q32[:, s % 2, P * t:P * (t + 1)],
                                                    k32[:, s % 2, HALF * half:HALF * (half + 1)],
                                                    start=True, stop=True)
                        last.then_inc(f_scores, 1)

                    def full_turn(n):
                        pe.wait_ge(f_norm, n + 1)
                        wait_for_bank(("turn", n))
                        for k in range(KT):
                            last = nc.tensor.transpose(work[:, k // QT, P * (k % QT):P * (k % QT + 1)],
                                                       p_full[:, n % 2, P * k:P * (k + 1)], ident)
                        last.then_inc(f_turned, 1)

                    def full_value(s, half, k):
                        m = s - HEAD_STAGES
                        if k == 0:
                            copied = KT * m + (half + 1) * QT
                            pe.wait_ge(f_copied[0], copied)
                            pe.wait_ge(f_copied[1], copied)
                            pe.wait_ge(bank_read, use["v1", s] + 1)
                            if 2 * m + half >= 1:
                                pe.wait_ge(f_out, 2 * m + half)
                        last = nc.tensor.matmul(outs[:, :], v_full[:, s % 2, k, :],
                                                pT_full[k // QT][:, k % QT, HALF * half:HALF * (half + 1)],
                                                start=k == 0, stop=k == KT - 1)
                        if k == KT - 1:
                            last.then_inc(f_pv, 1)

                    def do(kind, key):
                        if kind == "chunk":
                            chunk(*key)
                        elif kind == "tile":
                            score_tile(*key)
                        elif kind == "pair":
                            pair(key // 2, key % 2)
                        elif kind == "values" and key != -1:
                            values(key)

                    if not main:
                        pe.wait_ge(setup_loads, 64)
                        for kind, key in plan.order:
                            do(kind, key)
                        return
                    for slot in range(SLOTS):
                        for kind, key in plan.slot(slot):
                            do(kind, key)
                    values(SLOTS - 1)
                    pe.wait_ge(exp_done, 2 * SLOTS)
                    full_scores(HEAD_STAGES, 0)
                    full_scores(HEAD_STAGES, 1)
                    for s in range(HEAD_STAGES, STAGES):
                        for t in range(KT):
                            full_turn(KT * (s - HEAD_STAGES) + t)
                            if t + 2 < KT:
                                full_scores(s, t + 2)
                            for c in plan.fulls.get((s, t), []):
                                chunk(*c)
                            if t == 5 and s + 1 < STAGES:
                                if s == HEAD_STAGES:
                                    pe.wait_ge(o_turned, ROUNDS)
                                for k in range(KT):
                                    full_value(s, 0, k)
                        if s + 1 < STAGES:
                            full_scores(s + 1, 0)
                            for k in range(KT):
                                full_value(s, 1, k)
                            full_scores(s + 1, 1)
                    for kind, key in plan.tail():
                        if kind == "values":
                            full_value(STAGES - 1, key[1], key[2])
                        else:
                            do(kind, key)

            nc.all_engine_barrier(sems_to_clear=range(loop_sems[0].num, loop_sems[-1].num + 1))

        def image_at(tensor, n):
            return tensor[bass.ds(n, 1)].rearrange("o (p j) c -> (o p) j c", j=KT)

        def images(tensor, first):
            return [image_at(tensor, first + i) for i in range(PAIR)]

        run(Plan(main=False, then=True), images(x, 0), [])
        with nc.Fori(0, IMAGES // PAIR - 1) as step:
            run(Plan(main=True, then=True), images(x, step * PAIR + PAIR), images(out, step * PAIR))
        run(Plan(main=True, then=False), [], images(out, IMAGES - PAIR))


def kernel(**inputs):
    import numpy as np
    import concourse.bacc as _bacc
    from concourse import mybir as _mybir
    from concourse.bass_utils import run_bass_kernel_spmd as _run

    a = {n: np.asarray(v) for n, v in inputs.items()}
    C = CHANNELS

    def by_kind(w):
        return w.reshape(w.shape[0], HEADS, 3, HD).transpose(0, 2, 1, 3).reshape(w.shape[0], 3 * C)

    def padded(w):
        rows = np.zeros((HEADS, 2 * HD, C), w.dtype)
        rows[:, :HD] = w.reshape(HEADS, HD, C)
        return rows.reshape(2, P, C).transpose(1, 0, 2).reshape(P, 2 * C)

    none = np.zeros((C,), np.float32)
    b1 = by_kind(a["L1_conv_b_qkv"][None])[0]
    weights = np.concatenate([
        by_kind(a["L0_conv_w_qkv"]), by_kind(a["L1_conv_w_qkv"]),
        a["L2_conv_Wq"], a["L2_conv_Wk"], a["L2_conv_Wv"],
        a["L3_conv_wq"], a["L3_conv_wk"], a["L3_conv_wv"],
        padded(a["L0_conv_w_out"]), padded(a["L1_conv_w_out"]),
        a["L2_conv_Wp"], a["L3_conv_wp"]], axis=1)
    vectors = np.stack([
        a["L0_conv_gn_scale"], a["L0_conv_gn_bias"], none, none, a["L0_conv_b_out"],
        a["L1_conv_gn_scale"], a["L1_conv_gn_bias"], b1[:C], b1[C:2 * C], a["L1_conv_b_out"],
        a["L2_conv_ln_g"], a["L2_conv_ln_b"], a["L2_conv_bq"], a["L2_conv_bk"], a["L2_conv_bp"],
        a["L3_conv_gamma"], a["L3_conv_beta"], a["L3_conv_bq"], a["L3_conv_bk"], a["L3_conv_bp"]],
        axis=1)
    v_bias = np.stack([none, b1[2 * C:], a["L2_conv_bv"], a["L3_conv_bv"]])
    block8 = np.kron(np.eye(C // 8), np.full((8, 8), 1 / 8)).astype(np.float32)
    block4 = np.kron(np.eye(C // 4), np.full((4, 4), 1 / 4)).astype(np.float32)
    averages = np.concatenate([block8, block4,
                               np.eye(C, dtype=np.float32)], axis=1)
    arrays = {"x": a["x"].reshape(IMAGES, TOKENS, C), "weights": weights, "vectors": vectors,
              "v_bias": v_bias, "averages": averages}
    arrays = {n: np.ascontiguousarray(v) for n, v in arrays.items()}

    nc = _bacc.Bacc("TRN2", target_bir_lowering=False, num_devices=1)
    args = [nc.dram_tensor(n, v.shape, _mybir.dt.from_np(v.dtype), kind="ExternalInput").ap()
            for n, v in arrays.items()]
    out = nc.dram_tensor("out", (IMAGES, TOKENS, C), _mybir.dt.float32, kind="ExternalOutput").ap()
    attention_blocks(nc, *args, out)
    r = _run(nc, [arrays], core_ids=[0])
    return r.results[0]["out"].reshape(a["x"].shape)
```

```python
from contextlib import ExitStack

import numpy as np
import concourse.bass as bass
from concourse import mybir

P = 128
IMAGES, TOKENS, CHANNELS = 8, 1024, 128
PAIR = 2
STAGES = 8
NEXT = STAGES
HEAD_STAGES = 4
HEADS, HD = 8, 16
GROUP = 4
KT = TOKENS // P
HALF = TOKENS // 2
QT = KT // 2

ROUNDS = 4 * HEAD_STAGES
SLOTS = KT * ROUNDS
FULL_TILES = KT * (STAGES - HEAD_STAGES)
TILES = GROUP * KT
AHEAD = 3
FIRST_ROUNDS = 2
PROB_RING = 3
WORK_BANKS = 3
HEAD_SCALE = float(HD) ** -0.5
FULL_SCALE = float(CHANNELS) ** -0.5
GN_EPS, LN_EPS = 1e-5, 1e-3

Q_PART = [0, 0, 0, 1, 1, 2]
K_PART = [0, 1, 2, 0, 1, 0]
STACK = HD * len(Q_PART)
SHIFT = 2
TWO_ONES = float(np.uint32(0x3F803F80).view(np.float32))

F32, BF16 = mybir.dt.float32, mybir.dt.bfloat16
ALU = mybir.AluOpType
ACT = mybir.ActivationFunctionType
AX_X = mybir.AxisListType.X

GN_STEPS, LN_STEPS = 8, 8
LN_STAGES = [4, 5]
NO_BANK = ("stats", "apply", "lnstats0", "lnstats1", "lnapply0", "lnapply1",
           "second_k0", "second_k1", "second_q0", "second_q1")
TAKEN_BY_ACT = ("in", "turn", "back", "q", "k", "v", "turned")


def layer_of(s):
    return s % STAGES // 2


def projections(s):
    return [(n, s) for n in ("k0", "k1", "q0", "q1", "v0", "v1")]


def seconds(s):
    return [("second_" + n, s) for n, _ in projections(s)[:4]]


def head_chunks(then):
    at = {}

    def put(slot, *names):
        at.setdefault(slot, []).extend(names)

    put(2, ("in0", 1))
    put(3, ("in1", 1))
    for s in range(HEAD_STAGES):
        a = 4 * KT * s
        if s >= 1:
            put(a - 4, ("out0", s - 1))
            put(a + 4, ("out1", s - 1))
        if s + 1 < HEAD_STAGES:
            for i, n in enumerate(("stats", "gn1", "gn2", "apply")):
                put(a + 4 + i, (n, s + 1))
            for i, n in enumerate(seconds(s + 1)):
                put(a + 9 + i, n)
        else:
            for i, n in zip((5, 6, 7, 8, 10, 11, 12, 13),
                            ("turn0", "turn1", "lnstats0", "lnstats1", "lnapply0", "lnapply1",
                             "back0", "back1")):
                put(a + i, (n, s + 1))
            if then:
                for i, n in zip((14, 16, 18, 20, 22, 24), ("in0", "in1", "stats", "gn1", "gn2", "apply")):
                    put(a + i, (n, NEXT))
        for i, n in enumerate(projections(s + 1)):
            put(a + (8 if s + 1 < HEAD_STAGES else 14) + i, n)
    for r in range(FIRST_ROUNDS, ROUNDS):
        put(KT * (r - 1) + 5, ("shift", r))
    return at


def full_chunks(then):
    at = {}

    def put(s, t, *names):
        at.setdefault((s, t), []).extend(names)

    for s in range(HEAD_STAGES, STAGES):
        n = s + 1
        if s == HEAD_STAGES:
            put(s, -1, ("out0", s - 1))
            put(s, -0.5, ("out1", s - 1))
            put(s, 1, ("turn0", n), ("turn1", n))
            put(s, 1.5, ("lnstats0", n), ("lnstats1", n))
            put(s, 2.5, ("lnapply0", n))
            put(s, 3, ("lnapply1", n))
            put(s, 3.5, ("back0", n))
            put(s, 3.5, ("back1", n))
        else:
            put(s, 0, ("out0", s - 1))
            put(s, 3, ("out1", s - 1))
            if n < STAGES:
                put(s, 3.5, ("stats", n))
                put(s, 4, ("gn1", n))
                put(s, 4.5, ("gn2", n))
                put(s, 4.5, ("apply", n))
        if n < STAGES:
            for c, t in zip(projections(n), (5.5, 5.5, 5.5, 5.5, 6.5, 7.5)):
                put(s, t, c)
    if then:
        for c, t in zip(projections(NEXT), (-1, -1, -0.5, -0.5, 1, 2.5)):
            put(HEAD_STAGES, t, c)
        for c, t in zip(seconds(NEXT), (-0.5, 0, 0.5, 1)):
            put(HEAD_STAGES, t, c)
    put(STAGES - 1, 4.5, ("turned0", STAGES - 2))
    put(STAGES - 1, 5, ("turned1", STAGES - 2))
    return at


def tile_slots():
    at = {}
    for r in range(FIRST_ROUNDS, ROUNDS):
        slot = KT * (r - 1) - AHEAD
        if r == FIRST_ROUNDS:
            slots = [(slot + KT) * n // TILES for n in range(TILES)]
        elif r % 4 == 2:
            slots = [slot + t for t in range(KT) for _ in range(GROUP - 1 if t < QT else GROUP + 1)]
        else:
            slots = [slot + n // GROUP for n in range(TILES)]
        for n in range(TILES):
            at.setdefault(slots[n], []).append((r, n))
    return at


class Plan:

    FIRST = [("in0", NEXT), ("in1", NEXT), ("stats", NEXT), ("gn1", NEXT), ("gn2", NEXT),
             ("apply", NEXT), *projections(NEXT)[:3], seconds(NEXT)[0], projections(NEXT)[3],
             *seconds(NEXT)[1:], *projections(NEXT)[4:]]

    def __init__(self, main, then):
        self.main, self.then = main, then
        self.heads, self.fulls, self.tiles = head_chunks(then), full_chunks(then), tile_slots()
        self.order = []
        if main:
            for slot in range(SLOTS):
                self.order += self.slot(slot)
            self.full_order = self.one_head()
            self.order += self.full_order
        else:
            self.order += [("chunk", c) for c in self.FIRST]
            for r in self.next_rounds():
                self.order += [("tile", (r, n)) for n in range(TILES)]
                self.order.append(("chunk", ("shift", r)))
        self.stages = list(range(1, STAGES)) if main else []
        if then:
            self.stages.insert(HEAD_STAGES, NEXT)
        self.gn_stages = [s for s in self.stages if s not in LN_STAGES]
        self.head_stages = [s for s in self.stages if s < HEAD_STAGES or s == NEXT]
        self.rounds = (list(range(FIRST_ROUNDS, ROUNDS)) if main else []) + self.next_rounds()
        self.bank, self.before, self.use, self.takes, held, n = {}, {}, {}, {}, {}, 0
        for item in self.order:
            kind, key = item
            if kind == "chunk" and key[0] in NO_BANK or kind not in ("chunk", "tile", "turn"):
                continue
            bank = n % WORK_BANKS
            n += 1
            self.bank[item], self.before[item] = bank, held.get(bank)
            held[bank] = item
            if kind == "chunk":
                self.use[key] = len(self.use)
                self.takes[key] = sum(self.taker(c) == self.taker(key) for c in self.takes)

    def taker(self, chunk):
        return "act" if chunk[0].rstrip("01") in TAKEN_BY_ACT else "dve"

    def next_rounds(self):
        return [ROUNDS + r for r in range(FIRST_ROUNDS)] if self.then else []

    def slot(self, slot):
        tiles = [("tile", t) for t in self.tiles.get(slot, [])]
        chunks = [("chunk", c) for c in self.heads.get(slot, [])]
        return [("pair", 2 * slot), *tiles[0:2], ("pair", 2 * slot + 1), *tiles[2:3],
                ("values", slot - 1), *tiles[3:], *chunks]

    def one_head(self):
        first = [[("chunk", c) for c in self.fulls.get((HEAD_STAGES, t), [])] for t in (-1, -0.5)]
        order = [("values", SLOTS - 1), ("outputs", ROUNDS - 1), ("scores", 0), ("scores", 1),
                 *first[0], ("back", ROUNDS - 1), ("norm", 0), *first[1]]
        tiles = []
        for r in self.next_rounds():
            tiles += [("tile", (r, n)) for n in range(TILES)]
            tiles.append(("chunk", ("shift", r)))
        if self.then:
            tiles.insert(TILES + 3, tiles.pop(TILES))
        tiles_from, tiles_to = 5, FULL_TILES - 2

        def take(n):
            taken = tiles[:n]
            del tiles[:n]
            return taken

        for n in range(FULL_TILES):
            s, t = HEAD_STAGES + n // KT, n % KT
            share = -(-len(tiles) // (tiles_to - n)) if tiles_from <= n < tiles_to else 0
            order += [("turn", (n, 0)), ("turn", (n, 1))]
            if n + 1 < FULL_TILES:
                order.append(("norm", n + 1))
            order += take(share // 4)
            if n + 2 < FULL_TILES:
                order.append(("scores", n + 2))
            order += [("chunk", c) for c in self.fulls.get((s, t), [])]
            if t >= QT:
                steps = [(s, 0, 2 * (t - QT) + k) for k in range(2)]
            elif s > HEAD_STAGES:
                steps = [(s - 1, 1, k) for k in range(3 * t, min(3 * t + 3, KT))]
            else:
                steps = []
            left = share - share // 4
            for i, step in enumerate(steps):
                order += [("value", step), *take(left // 3)]
            order += [("chunk", c) for c in self.fulls.get((s, t + 0.5), [])]
            if steps:
                order += take(left - len(steps) * (left // 3))
        s = STAGES - 1
        for k in range(KT):
            order.append(("value", (s, 1, k)))
            if k in (1, 4):
                order.append(("chunk", ("out0" if k == 1 else "turned0", s)))
        return order + [("chunk", ("out1", s)), ("chunk", ("turned1", s))]

    def tile_ordinal(self, r, n):
        return TILES * self.rounds.index(r) + n


def attention_blocks(nc, x, weights, vectors, averages, out):
    with ExitStack() as ctx:
        def sb(name, shape, dt=F32):
            return ctx.enter_context(nc.sbuf_tensor(name, shape, dt))

        def psum(name, shape, dt=F32):
            return ctx.enter_context(nc.psum_tensor(name, shape, dt))

        loop_sems = []

        def sem(name):
            s = ctx.enter_context(nc.semaphore(name))
            loop_sems.append(s)
            return s

        w = sb("w", [P, weights.shape[1]])
        vec = sb("vec", [P, vectors.shape[1]])
        qbias = sb("qbias", [P, 4])
        obias = sb("obias", [P, 4])
        avg = sb("avg", [P, 3 * P])
        minus_half = sb("minus_half", [P, KT])
        xin = sb("xin", [P, PAIR, KT, CHANNELS])
        x_next = sb("x_next", [P, TOKENS])
        xT = sb("xT", [P, PAIR, TOKENS])
        hT = sb("hT", [P, PAIR, TOKENS])
        xtok = sb("xtok", [P, KT, CHANNELS])
        q32 = sb("q32", [P, PAIR, TOKENS])
        k32 = sb("k32", [P, PAIR, TOKENS])
        q_parts = sb("q_parts", [P, 3, 2, HALF], BF16)
        k_parts = sb("k_parts", [P, 3, 2, HALF], BF16)
        rest = sb("rest", [P, 2, HALF])
        q_stack = sb("q_stack", [P, PAIR * HEADS * TOKENS], BF16)
        k_stack = sb("k_stack", [P, PAIR * HEADS * TOKENS], BF16)
        v_heads = sb("v_heads", [P, PAIR, KT, HEADS, 2 * HD])
        v_full = sb("v_full", [P, PAIR, KT, CHANNELS])
        probs = sb("probs", [P, PROB_RING, GROUP, HALF])
        o_turn = sb("o_turn", [P, 2, HALF // 32, 32])
        o_scale = sb("o_scale", [P, 2, HALF // 32, 32])
        o_inv = sb("o_inv", [P, 2, HALF // 32])
        oT = sb("oT", [P, 2, TOKENS])
        part_max = sb("part_max", [P, 2, TILES])
        neg_max = sb("neg_max", [P, 2, TILES // 2])
        shift_parts = sb("shift_parts", [TILES // 2, 2, P], BF16)
        stats = sb("stats", [P, KT, nc.vector.BN_STATS_DIM])
        mv = sb("mv", [P, KT, 2])
        gmean = sb("gmean", [P, 1])
        dev = sb("dev", [P, 1])
        var_in = sb("var_in", [P, 1])
        var_eps = sb("var_eps", [P, KT])
        rstd = sb("rstd", [P, KT])
        gscale = sb("gscale", [P, 1])
        gshift = sb("gshift", [P, 2])
        neg_max1 = sb("neg_max1", [P, 4])
        sum1 = sb("sum1", [P, 4])
        inv1 = sb("inv1", [P, 4])

        qs = q_stack[:, :].rearrange("p (i a h t) -> p i a h t", i=PAIR, a=2, h=HEADS)
        ks = k_stack[:, :].rearrange("p (i a h t) -> p i a h t", i=PAIR, a=2, h=HEADS)
        p_full = probs[:, 0, :, :].rearrange("p (n a) k -> p n (a k)", n=2)
        pT_full = [q_stack[:, HEADS * TOKENS:].bitcast(F32).rearrange("p (k q) -> p k q", k=QT),
                   probs[:, 1:3, :, :].rearrange("p n (m a) k -> p (n m) (a k)", m=2)]

        ident = avg[:, 2 * P:3 * P]
        group_avg = {0: avg[:, 0:P], 1: avg[:, P:2 * P], 3: avg[:, P:2 * P]}

        def w_of(layer, n):
            return w[:, (3 * layer + n) * P:(3 * layer + n + 1) * P]

        def w_out(layer, g=0):
            n = 12 + (2 * layer + g if layer < 2 else 2 + layer)
            return w[:, n * P:(n + 1) * P]

        def vec_of(layer, n):
            return vec[:, 5 * layer + n:5 * layer + n + 1]

        pairs = psum("pairs", [P, 2, 2, HALF])
        outs = psum("outs", [P, HALF])
        work = psum("work", [P, WORK_BANKS, HALF])

        scratch = {n: nc.dram_tensor(f"{n}_scratch", [3, 2 * HEADS, HD, HALF], BF16, kind="Internal").ap()
                   for n in "qk"}

        averages_loaded = sem("averages_loaded")
        vectors_loaded = sem("vectors_loaded")
        weights_loaded = sem("weights_loaded")
        value_bias = sem("value_bias")
        qbias_ready = sem("qbias_ready")
        image_loaded = [sem("image0_loaded"), sem("image1_loaded")]
        bank_full = sem("bank_full")
        taken_by = {n: sem(f"taken_by_{n}") for n in ("act", "dve")}
        gn_step = sem("gn_step")
        ln_step = sem("ln_step")
        rstd_ready = sem("rstd_ready")
        h_ready = sem("h_ready")
        rest_ready = sem("rest_ready")
        second_ready = sem("second_ready")
        third_ready = sem("third_ready")
        parts_out = {n: sem(f"{n}_parts_out") for n in "qk"}
        stacked = {n: sem(f"{n}_stacked") for n in "qk"}
        tile_full = sem("tile_full")
        tile_max = sem("tile_max")
        max_ready = sem("max_ready")
        shift_hi = sem("shift_hi")
        shift_in = sem("shift_in")
        pair_full = sem("pair_full")
        exp_done = sem("exp_done")
        pv_done = sem("pv_done")
        o_turned = sem("o_turned")
        o_inverse = sem("o_inverse")
        o_scaled = sem("o_scaled")
        o_ready = sem("o_ready")
        f_scores = sem("f_scores")
        f_max = sem("f_max")
        f_exp = sem("f_exp")
        f_inv = sem("f_inv")
        f_norm = sem("f_norm")
        f_turned = sem("f_turned")
        f_copied = [sem("f_copied_lo"), sem("f_copied_hi")]
        f_pv = sem("f_pv")
        f_out = sem("f_out")
        y_stored = sem("y_stored")

        def run(plan, loads, stores):
            use = plan.use
            main, then = plan.main, plan.then

            def half_of(name):
                return int(name[-1]) if name[-1] in "01" else 0

            def kind_of(name):
                return name if name in ("gn1", "gn2") else name.rstrip("01")

            def x_of(s):
                return x_next[:, :] if s == NEXT else xT[:, s % 2, :]

            def tiles_of(half):
                return slice(QT * half, QT * (half + 1))

            def result_of(s):
                return xtok[:, :, :] if s % 2 == 0 else hT[:, 1, :].rearrange("p (j c) -> p j c", j=KT)

            def h_of(s):
                return xtok[:, :, :].rearrange("p j c -> p (j c)") if s == NEXT else hT[:, s % 2, :]

            def tokens_of(s):
                return xin[:, 0, :, :] if s == LN_STAGES[1] else xtok[:, :, :]

            def whole_of(n, s):
                return {"q": q32, "k": k32}[n][:, 1 if s == NEXT else s % 2, :]

            def parts_of(name):
                return k_parts if name[0] == "k" else q_parts

            def taken(*chunk):
                return taken_by[plan.taker(chunk)], plan.takes[chunk] + 1

            def bank_of(*chunk):
                return work[:, plan.bank["chunk", chunk], :]

            with nc.Block() as block:
                @block.sync
                def _(sp):
                    def load(i):
                        sp.dma_start(xin[:, i, :, :], loads[i]).then_inc(image_loaded[i], 16)

                    def stack(s):
                        n_th = plan.head_stages.index(s)
                        for i, (n, parts) in enumerate((("k", k_parts), ("q", q_parts))):
                            sp.wait_ge(third_ready, 4 * n_th + 2 * (i + 1))
                            for j in range(3):
                                to = scratch[n][j].rearrange("(a h) r t -> (h r) a t", a=2)
                                sp.dma_start(to, parts[:, j, :, :]).then_inc(parts_out[n], 16)
                        for n, to, which in (("k", ks, K_PART), ("q", qs, Q_PART)):
                            sp.wait_ge(parts_out[n], 48 * (n_th + 1))
                            for j, part in enumerate(which):
                                rows = to[HD * j:HD * (j + 1), s % 2, :, :, :]
                                sp.dma_start(rows.rearrange("r a h t -> r (a h) t"),
                                             scratch[n][part].rearrange("m r t -> r m t")
                                             ).then_inc(stacked[n], 16)

                    def shift(r):
                        first = GROUP * (r // 2 % 2)
                        sp.wait_ge(*taken("shift", r))
                        for j in range(SHIFT):
                            row = qs[STACK + j:STACK + j + 1, r // 4 % 2, r % 2, first:first + GROUP, :]
                            sp.dma_start(row.rearrange("o h (n q) -> o (h n) q", n=QT),
                                         shift_parts[:, j, :]).then_inc(shift_in, 16)

                    def store(i, half):
                        sp.wait_ge(*taken(f"turned{half}", STAGES - PAIR + i))
                        sp.dma_start(stores[i][:, tiles_of(half), :], result_of(i)[:, tiles_of(half), :]
                                     ).then_inc(y_stored, 16)

                    if not main:
                        load(0)
                        sp.dma_start(avg[:, :], averages).then_inc(averages_loaded, 16)
                        sp.dma_start(vec[:, :], vectors).then_inc(vectors_loaded, 16)
                        sp.dma_start(w[:, :], weights).then_inc(weights_loaded, 16)
                        load(1)
                        stack(NEXT)
                        for r in plan.rounds:
                            shift(r)
                        sp.wait_ge(shift_in, 32 * len(plan.rounds))
                        sp.wait_ge(image_loaded[1], 16)
                        return
                    if then:
                        sp.wait_ge(*taken("in1", 1))
                        load(0)
                        load(1)
                    for r in range(FIRST_ROUNDS, ROUNDS):
                        if r % 4 == 3 and r // 4 + 1 < HEAD_STAGES:
                            stack(r // 4 + 1)
                        shift(r)
                    if then:
                        stack(NEXT)
                    for kind, key in plan.full_order:
                        if kind == "chunk" and key[0] == "shift":
                            shift(key[1])
                        elif kind == "chunk" and kind_of(key[0]) == "turned":
                            store(key[1] - (STAGES - PAIR), half_of(key[0]))
                    if then:
                        sp.wait_ge(shift_in, 32 * len(plan.rounds))
                    sp.wait_ge(y_stored, 16 * 2 * PAIR)

                @block.gpsimd
                def _(pool):
                    def inverse_root(s):
                        n = KT if s in LN_STAGES else 1
                        if s in LN_STAGES:
                            pool.wait_ge(ln_step, LN_STEPS * LN_STAGES.index(s) + 6)
                        else:
                            pool.wait_ge(*taken("gn2", s))
                        nc.gpsimd.tensor_tensor(rstd[:, 0:n], var_eps[:, 0:n], minus_half[:, 0:n],
                                                ALU.pow).then_inc(rstd_ready, 1)

                    def split_rest(s, i):
                        name = projections(s)[i][0]
                        n = 4 * plan.head_stages.index(s) + i
                        pool.wait_ge(*taken(name, s))
                        if n >= 2:
                            pool.wait_ge(third_ready, n - 1)
                        nc.gpsimd.tensor_tensor(rest[:, n % 2, :],
                                                whole_of(name[0], s)[:, HALF * (i % 2):HALF * (i % 2 + 1)],
                                                parts_of(name)[:, 0, i % 2, :], ALU.subtract
                                                ).then_inc(rest_ready, 1)

                    def split_third(s, i):
                        name = projections(s)[i][0]
                        n = 4 * plan.head_stages.index(s) + i
                        pool.wait_ge(second_ready, n + 1)
                        nc.gpsimd.tensor_tensor(parts_of(name)[:, 2, i % 2, :], rest[:, n % 2, :],
                                                parts_of(name)[:, 1, i % 2, :], ALU.subtract
                                                ).then_inc(third_ready, 1)

                    def split(s):
                        split_rest(s, 0)
                        for i in range(1, 4):
                            split_rest(s, i)
                            split_third(s, i - 1)
                        split_third(s, 3)

                    def scale_outputs(r):
                        pool.wait_ge(o_inverse, r + 1)
                        if r >= 2:
                            pool.wait_ge(o_ready, r - 1)
                        inv = o_inv[:, r % 2, :].unsqueeze(2).to_broadcast([P, HALF // 32, 32])
                        nc.gpsimd.tensor_tensor(o_scale[:, r % 2, :, :], o_turn[:, r % 2, :, :], inv,
                                                ALU.mult).then_inc(o_scaled, 1)

                    if not main:
                        inverse_root(NEXT)
                        split(NEXT)
                        return
                    for s in range(HEAD_STAGES):
                        if s >= 1:
                            scale_outputs(4 * s - 1)
                        inverse_root(s + 1)
                        scale_outputs(4 * s)
                        if s + 1 < HEAD_STAGES:
                            split(s + 1)
                        scale_outputs(4 * s + 1)
                        if s == HEAD_STAGES - 1 and then:
                            inverse_root(NEXT)
                        scale_outputs(4 * s + 2)
                    scale_outputs(ROUNDS - 1)
                    if then:
                        split(NEXT)
                    for s in range(HEAD_STAGES + 1, STAGES):
                        inverse_root(s)

                @block.scalar
                def _(act):
                    def chunk(name, s):
                        kind, half, layer = kind_of(name), half_of(name), layer_of(s)
                        cols = slice(HALF * half, HALF * (half + 1))
                        if kind == "apply":
                            act.wait_ge(gn_step, GN_STEPS * (plan.gn_stages.index(s) + 1))
                            nc.scalar.activation(h_of(s), x_of(s), ACT.Identity, bias=gshift[:, 1:2],
                                                 scale=gscale[:, :]).then_inc(h_ready, 1)
                        elif kind in ("second_k", "second_q"):
                            n = 4 * plan.head_stages.index(s) + 2 * (kind[-1] == "q") + half
                            act.wait_ge(rest_ready, n + 1)
                            nc.scalar.copy(parts_of(kind[-1])[:, 1, half, :], rest[:, n % 2, :]
                                           ).then_inc(second_ready, 1)
                        if kind not in TAKEN_BY_ACT + ("shift",):
                            return
                        bank = bank_of(name, s)
                        by_token = bank.rearrange("p (j c) -> p j c", c=CHANNELS)
                        if kind == "shift" and s > plan.rounds[0]:
                            act.wait_ge(shift_in, 32 * plan.rounds.index(s))
                        act.wait_ge(bank_full, use[name, s] + 1)
                        if kind == "in":
                            nc.scalar.copy(x_of(s)[:, cols], bank).then_inc(taken_by["act"], 1)
                        elif kind == "turn":
                            nc.scalar.copy(tokens_of(s)[:, tiles_of(half), :], by_token).then_inc(taken_by["act"], 1)
                        elif kind == "back":
                            nc.scalar.activation(hT[:, s % 2, cols], bank, ACT.Identity,
                                                 bias=vec_of(layer, 1), scale=vec_of(layer, 0)
                                                 ).then_inc(taken_by["act"], 1)
                        elif kind == "v":
                            if s in plan.head_stages:
                                to = v_heads[:, s % 2, tiles_of(half), :, 0:HD]
                                by_token = by_token.rearrange("p j (h d) -> p j h d", h=HEADS)
                            else:
                                to = v_full[:, s % 2, tiles_of(half), :]
                            nc.scalar.copy(to, by_token).then_inc(taken_by["act"], 1)
                        elif kind in ("q", "k"):
                            parts, bias, scale = k_parts, vec_of(layer, 3), 1.0
                            if kind == "q":
                                parts, bias = q_parts, qbias[:, layer:layer + 1]
                                scale = 1.0 if layer < 2 else FULL_SCALE
                            last = nc.scalar.activation(whole_of(kind, s)[:, cols], bank, ACT.Identity,
                                                        bias=bias, scale=scale)
                            if s in plan.head_stages:
                                last = nc.scalar.activation(parts[:, 0, half, :], bank, ACT.Identity,
                                                            bias=bias, scale=scale)
                            last.then_inc(taken_by["act"], 1)
                        elif kind == "shift":
                            nc.scalar.copy(shift_parts[:, 0, :], bank[0:TILES // 2, 0:P]
                                           ).then_inc(shift_hi, 1)
                        elif kind == "turned":
                            nc.scalar.copy(result_of(s)[:, tiles_of(half), :], by_token
                                           ).then_inc(taken_by["act"], 1)

                    def exp(u, n):
                        t = 2 * u + n
                        if n == 0 and u >= PROB_RING:
                            act.wait_ge(pv_done, u - PROB_RING + 1)
                        act.wait_ge(pair_full, t + 1)
                        nc.scalar.activation(probs[:, u % PROB_RING, 2 * n:2 * n + 2, :],
                                             pairs[:, t % 2, :, :], ACT.Exp, scale=HEAD_SCALE
                                             ).then_inc(exp_done, 1)

                    def full_exp(n):
                        act.wait_ge(f_max, n + 1)
                        if n >= 2:
                            act.wait_ge(f_turned, 2 * (n - 1))
                        nc.scalar.activation(p_full[:, n % 2, :],
                                             pairs[:, n % 2, :, :].rearrange("p a k -> p (a k)"), ACT.Exp,
                                             bias=neg_max1[:, n % 4:n % 4 + 1],
                                             accum_out=sum1[:, n % 4:n % 4 + 1]).then_inc(f_exp, 1)

                    def full_copy(n):
                        act.wait_ge(f_turned, 2 * n + 1)
                        m, t = n // KT, n % KT
                        if m >= 1 and t % QT == 0:
                            act.wait_ge(f_pv, 2 * m - 1 + t // QT)
                        nc.scalar.copy(pT_full[0][:, :, P * t:P * (t + 1)],
                                       work[:, plan.bank["turn", (n, 0)], :].rearrange(
                                           "p (k q) -> p k q", q=P)).then_inc(f_copied[0], 1)

                    def full_out(s, half):
                        act.wait_ge(f_pv, 2 * (s - HEAD_STAGES) + half + 1)
                        nc.scalar.copy(oT[:, 0, HALF * half:HALF * (half + 1)], outs[:, :]
                                       ).then_inc(f_out, 1)

                    if not main:
                        act.wait_ge(qbias_ready, 4)
                        for kind, key in plan.order:
                            if kind == "chunk":
                                chunk(*key)
                        return
                    for slot in range(SLOTS):
                        exp(slot, 0)
                        exp(slot, 1)
                        for c in plan.heads.get(slot, []):
                            chunk(*c)
                    for kind, key in plan.full_order:
                        if kind == "chunk":
                            chunk(*key)
                        elif kind == "scores":
                            full_exp(key)
                        elif kind == "turn" and key[1] == 0:
                            full_copy(key[0])
                        elif kind == "value" and key[2] == KT - 1:
                            full_out(key[0], key[1])

                @block.vector
                def _(dve):
                    def chunk(name, s):
                        kind, half, layer = kind_of(name), half_of(name), layer_of(s)
                        cols = slice(HALF * half, HALF * (half + 1))
                        if s in plan.gn_stages:
                            step0 = GN_STEPS * plan.gn_stages.index(s)
                        if kind == "stats":
                            source = ("in1", s) if s in (1, NEXT) else ("out1", s - 2)
                            dve.wait_ge(*taken(*source))
                            for t in range(2):
                                nc.vector.bn_stats(stats[:, t, :], x_of(s)[:, HALF * t:HALF * (t + 1)]
                                                   ).then_inc(gn_step, 1)
                            dve.wait_ge(gn_step, step0 + 2)
                            nc.vector.bn_aggr(mv[:, 0, :], stats[:, 0:2, :]).then_inc(gn_step, 1)
                        elif kind == "gn1":
                            dve.wait_ge(bank_full, use[name, s] + 1)
                            nc.vector.tensor_copy(gmean[:, :], bank_of(name, s)[:, 0:1]
                                                  ).then_inc(taken_by["dve"], 1)
                            dve.wait_ge(*taken(name, s))
                            nc.vector.tensor_tensor(dev[:, :], mv[:, 0, 0:1], gmean[:, :], ALU.subtract
                                                    ).then_inc(gn_step, 1)
                            dve.wait_ge(gn_step, step0 + 4)
                            nc.vector.scalar_tensor_tensor(var_in[:, :], dev[:, :], dev[:, :],
                                                           mv[:, 0, 1:2], ALU.mult, ALU.add
                                                           ).then_inc(gn_step, 1)
                        elif kind == "gn2":
                            dve.wait_ge(bank_full, use[name, s] + 1)
                            nc.vector.tensor_scalar(var_eps[:, 0:1], bank_of(name, s)[:, 0:1], GN_EPS,
                                                    None, ALU.add).then_inc(taken_by["dve"], 1)
                        elif kind == "apply":
                            dve.wait_ge(rstd_ready, plan.stages.index(s) + 1)
                            nc.vector.tensor_tensor(gscale[:, :], rstd[:, 0:1], vec_of(layer, 0),
                                                    ALU.mult).then_inc(gn_step, 1)
                            dve.wait_ge(gn_step, step0 + 6)
                            nc.vector.tensor_tensor(gshift[:, 0:1], gmean[:, :], gscale[:, :], ALU.mult
                                                    ).then_inc(gn_step, 1)
                            dve.wait_ge(gn_step, step0 + 7)
                            nc.vector.tensor_tensor(gshift[:, 1:2], vec_of(layer, 1), gshift[:, 0:1],
                                                    ALU.subtract).then_inc(gn_step, 1)
                        elif kind == "lnstats":
                            step = LN_STEPS * LN_STAGES.index(s) + 3 * half
                            dve.wait_ge(*taken(f"turn{half}", s))
                            for j in range(QT * half, QT * (half + 1)):
                                last = nc.vector.bn_stats(stats[:, j, :], tokens_of(s)[:, j, :])
                            last.then_inc(ln_step, 1)
                            dve.wait_ge(ln_step, step + 1)
                            for j in range(QT * half, QT * (half + 1)):
                                last = nc.vector.bn_aggr(mv[:, j, :], stats[:, j, :])
                            last.then_inc(ln_step, 1)
                            dve.wait_ge(ln_step, step + 2)
                            nc.vector.tensor_scalar(var_eps[:, tiles_of(half)], mv[:, tiles_of(half), 1],
                                                    LN_EPS, None, ALU.add).then_inc(ln_step, 1)
                        elif kind == "lnapply":
                            if half == 0:
                                dve.wait_ge(rstd_ready, plan.stages.index(s) + 1)
                            for j in range(QT * half, QT * (half + 1)):
                                token = tokens_of(s)[:, j, :]
                                last = nc.vector.tensor_scalar(token, token,
                                                               mv[:, j, 0:1], rstd[:, j:j + 1],
                                                               ALU.subtract, ALU.mult)
                            last.then_inc(ln_step, 1)
                        elif kind == "shift":
                            dve.wait_ge(shift_hi, plan.rounds.index(s) + 1)
                            nc.vector.tensor_tensor(shift_parts[:, 1, :],
                                                    bank_of(name, s)[0:TILES // 2, 0:P],
                                                    shift_parts[:, 0, :], ALU.subtract
                                                    ).then_inc(taken_by["dve"], 1)
                        elif kind == "out":
                            skip = hT[:, s % 2, :] if layer == 1 else x_of(s)
                            if s == 0:
                                skip = x_next[:, :]
                            dve.wait_ge(bank_full, use[name, s] + 1)
                            nc.vector.scalar_tensor_tensor(xT[:, s % 2, cols], bank_of(name, s),
                                                           obias[:, layer:layer + 1], skip[:, cols], ALU.add,
                                                           ALU.add).then_inc(taken_by["dve"], 1)

                    def tile_maximum(r, n):
                        t = plan.tile_ordinal(r, n)
                        dve.wait_ge(tile_full, t + 1)
                        nc.vector.tensor_reduce(part_max[:, r % 2, n:n + 1],
                                                work[:, plan.bank["tile", (r, n)], :], AX_X, ALU.max,
                                                negate=True).then_inc(tile_max, 1)
                        if n == TILES - 1:
                            dve.wait_ge(tile_max, t + 1)
                            nc.vector.tensor_reduce(neg_max[:, r % 2, :],
                                                    part_max[:, r % 2, :].rearrange(
                                                        "p (n a) -> p n a", a=2), AX_X, ALU.min
                                                    ).then_inc(max_ready, 1)

                    def turn_outputs(r):
                        dve.wait_ge(pv_done, KT * (r + 1))
                        if r >= 2:
                            dve.wait_ge(o_scaled, r - 1)
                        nc.vector.transpose(o_turn[:, r % 2, :, :].rearrange("p b c -> p (b c)"),
                                            outs[:, :]).then_inc(o_turned, 1)
                        dve.wait_ge(o_turned, r + 1)
                        nc.vector.reciprocal(o_inv[:, r % 2, :], o_turn[:, r % 2, :, HD]
                                             ).then_inc(o_inverse, 1)

                    def turn_back(r):
                        half = slice(HALF * (r % 2), HALF * (r % 2 + 1))
                        dve.wait_ge(o_scaled, r + 1)
                        nc.vector.transpose(oT[:, r // 2 % 2, half],
                                            o_scale[:, r % 2, :, :].rearrange("p b c -> p (b c)")
                                            ).then_inc(o_ready, 1)

                    def full_max(n):
                        dve.wait_ge(f_scores, n + 1)
                        nc.vector.tensor_reduce(neg_max1[:, n % 4:n % 4 + 1],
                                                pairs[:, n % 2, :, :].rearrange("p a k -> p (a k)"),
                                                AX_X, ALU.max, negate=True).then_inc(f_max, 1)

                    def full_normalise(n):
                        dve.wait_ge(f_exp, n + 1)
                        nc.vector.reciprocal(inv1[:, n % 4:n % 4 + 1], sum1[:, n % 4:n % 4 + 1]
                                             ).then_inc(f_inv, 1)
                        dve.wait_ge(f_inv, n + 1)
                        nc.vector.tensor_scalar(p_full[:, n % 2, :], p_full[:, n % 2, :],
                                                inv1[:, n % 4:n % 4 + 1], None, ALU.mult
                                                ).then_inc(f_norm, 1)

                    def full_copy(n):
                        dve.wait_ge(f_turned, 2 * n + 2)
                        m, t = n // KT, n % KT
                        if m >= 1 and t % QT == 0:
                            dve.wait_ge(f_pv, 2 * m - 1 + t // QT)
                        nc.vector.tensor_copy(pT_full[1][:, :, P * t:P * (t + 1)],
                                              work[:, plan.bank["turn", (n, 1)], :].rearrange(
                                                  "p (k q) -> p k q", q=P)).then_inc(f_copied[1], 1)

                    if not main:
                        nc.vector.memset(minus_half[:, :], -0.5)
                        dve.wait_ge(vectors_loaded, 16)
                        for layer in range(4):
                            scale = 1.0 if layer < 2 else FULL_SCALE
                            nc.vector.tensor_scalar(qbias[:, layer:layer + 1], vec_of(layer, 2), scale,
                                                    None, ALU.mult).then_inc(qbias_ready, 1)
                        for c in plan.FIRST:
                            chunk(*c)
                        nc.vector.memset(v_heads[:, :, :, :, HD:2 * HD], 1.0)
                        nc.vector.memset(k_stack[STACK:STACK + SHIFT, :].bitcast(F32), TWO_ONES)
                        dve.wait_ge(value_bias, 1)
                        nc.vector.tensor_copy(obias[:, 0:1], vec_of(0, 4))
                        nc.vector.tensor_tensor(obias[:, 1:4], outs[:, 1:4], vec[:, 9:20:5], ALU.add)
                        for kind, key in plan.order[len(plan.FIRST):]:
                            if kind == "chunk":
                                chunk(*key)
                            elif kind == "tile":
                                tile_maximum(*key)
                        return
                    for slot in range(SLOTS):
                        r = slot // KT - 1
                        if r >= 0 and slot % KT == 1:
                            turn_outputs(r)
                        if r >= 0 and slot % KT == (7 if r % 4 < 2 else 3):
                            turn_back(r)
                        for t in plan.tiles.get(slot, []):
                            tile_maximum(*t)
                        for c in plan.heads.get(slot, []):
                            chunk(*c)
                    for kind, key in plan.full_order:
                        if kind == "chunk":
                            chunk(*key)
                        elif kind == "tile":
                            tile_maximum(*key)
                        elif kind == "scores":
                            full_max(key)
                        elif kind == "norm":
                            full_normalise(key)
                        elif kind == "turn" and key[1] == 1:
                            full_copy(key[0])
                        elif kind == "outputs":
                            turn_outputs(key)
                        elif kind == "back":
                            turn_back(key)

                @block.tensor
                def _(pe):
                    def wait_for_bank(item):
                        if plan.before[item] is not None:
                            kind, key = plan.before[item]
                            if kind == "tile":
                                pe.wait_ge(tile_max, plan.tile_ordinal(*key) + 1)
                            elif kind == "turn":
                                pe.wait_ge(f_copied[key[1]], key[0] + 1)
                            else:
                                pe.wait_ge(*taken(*key))

                    def chunk(name, s):
                        kind, half, layer = kind_of(name), half_of(name), layer_of(s)
                        if name in NO_BANK:
                            return
                        cols = slice(HALF * half, HALF * (half + 1))
                        bank = bank_of(name, s)
                        wait_for_bank(("chunk", (name, s)))
                        if kind == "in":
                            if s == NEXT:
                                pe.wait_ge(image_loaded[0], 16)
                            for j in range(QT):
                                last = nc.tensor.transpose(bank[:, P * j:P * (j + 1)],
                                                           xin[:, s % 2, QT * half + j, :], ident)
                        elif kind == "gn1":
                            pe.wait_ge(gn_step, GN_STEPS * plan.gn_stages.index(s) + 3)
                            last = nc.tensor.matmul(bank[:, 0:1], group_avg[layer], mv[:, 0, 0:1],
                                                    start=True, stop=True)
                        elif kind == "gn2":
                            pe.wait_ge(gn_step, GN_STEPS * plan.gn_stages.index(s) + 5)
                            last = nc.tensor.matmul(bank[:, 0:1], group_avg[layer], var_in[:, :],
                                                    start=True, stop=True)
                        elif kind in ("q", "k"):
                            if not main:
                                pe.wait_ge(weights_loaded, 16)
                            if s in plan.gn_stages:
                                pe.wait_ge(h_ready, plan.gn_stages.index(s) + 1)
                            last = nc.tensor.matmul(bank, w_of(layer, "qk".index(kind)),
                                                    h_of(s)[:, cols], start=True, stop=True)
                        elif kind == "v":
                            for j in range(QT):
                                t = QT * half + j
                                last = nc.tensor.matmul(bank[:, P * j:P * (j + 1)],
                                                        h_of(s)[:, P * t:P * (t + 1)], w_of(layer, 2),
                                                        start=True, stop=True)
                        elif kind == "shift":
                            pe.wait_ge(max_ready, plan.rounds.index(s) + 1)
                            last = nc.tensor.transpose(bank[0:TILES // 2, 0:P], neg_max[:, s % 2, :],
                                                       ident)
                        elif kind == "out":
                            if s < HEAD_STAGES:
                                pe.wait_ge(o_ready, 4 * s + 2 + half + 1)
                                for g in range(2):
                                    last = nc.tensor.matmul(bank, w_out(layer, g), oT[:, g, cols],
                                                            start=g == 0, stop=g == 1)
                            else:
                                pe.wait_ge(f_out, 2 * (s - HEAD_STAGES) + half + 1)
                                last = nc.tensor.matmul(bank, w_out(layer), oT[:, 0, cols],
                                                        start=True, stop=True)
                        elif kind in ("turn", "turned"):
                            pe.wait_ge(*taken(f"out{half}", s - 2 if kind == "turn" else s))
                            for j in range(QT):
                                t = QT * half + j
                                last = nc.tensor.transpose(bank[:, P * j:P * (j + 1)],
                                                           xT[:, s % 2, P * t:P * (t + 1)], ident)
                        elif kind == "back":
                            pe.wait_ge(ln_step, LN_STEPS * LN_STAGES.index(s) + 7 + half)
                            for j in range(QT):
                                last = nc.tensor.transpose(bank[:, P * j:P * (j + 1)],
                                                           tokens_of(s)[:, QT * half + j, :], ident)
                        last.then_inc(bank_full, 1)

                    def score_tile(r, n):
                        i, head = r // 4 % 2, GROUP * (r // 2 % 2) + n // KT
                        t, keys = n // 2 % QT, n % 2
                        if n == 0 and r % 4 == 0:
                            stage = r // 4 if r < ROUNDS else NEXT
                            for name in "kq":
                                pe.wait_ge(stacked[name], 96 * (plan.head_stages.index(stage) + 1))
                        wait_for_bank(("tile", (r, n)))
                        nc.tensor.matmul(work[:, plan.bank["tile", (r, n)], :],
                                         qs[0:STACK, i, r % 2, head, P * t:P * (t + 1)],
                                         ks[0:STACK, i, keys, head, :],
                                         start=True, stop=True).then_inc(tile_full, 1)

                    def pair(u, n):
                        t, r, key = 2 * u + n, u // KT, u % KT
                        if key == 0 and n == 0 and r >= FIRST_ROUNDS:
                            pe.wait_ge(shift_in, 32 * (plan.rounds.index(r) + 1))
                        if t >= 2:
                            pe.wait_ge(exp_done, t - 1)
                        for h in range(2):
                            head = GROUP * (r // 2 % 2) + 2 * n + h
                            last = nc.tensor.matmul(
                                pairs[:, t % 2, h, :],
                                ks[0:STACK + SHIFT, r // 4 % 2, key // QT, head,
                                   P * (key % QT):P * (key % QT + 1)],
                                qs[0:STACK + SHIFT, r // 4 % 2, r % 2, head, :], start=True, stop=True)
                        last.then_inc(pair_full, 1)

                    def values(u):
                        r, key = u // KT, u % KT
                        pe.wait_ge(exp_done, 2 * (u + 1))
                        if key == 0 and r > 0:
                            pe.wait_ge(o_turned, r)
                        for h in range(GROUP):
                            last = nc.tensor.matmul(outs[2 * HD * h:2 * HD * (h + 1), :],
                                                    v_heads[:, r // 4 % 2, key,
                                                            GROUP * (r // 2 % 2) + h, :],
                                                    probs[:, u % PROB_RING, h, :],
                                                    start=key == 0, stop=key == KT - 1)
                        last.then_inc(pv_done, 1)

                    def full_scores(n):
                        s, t = HEAD_STAGES + n // KT, n % KT
                        if t == 0:
                            pe.wait_ge(*taken("q1", s))
                        if n < 2:
                            pe.wait_ge(exp_done, 2 * SLOTS - 1 + n)
                        else:
                            pe.wait_ge(f_exp, n - 1)
                        for half in range(2):
                            last = nc.tensor.matmul(pairs[:, n % 2, half, :],
                                                    q32[:, s % 2, P * t:P * (t + 1)],
                                                    k32[:, s % 2, HALF * half:HALF * (half + 1)],
                                                    start=True, stop=True)
                        last.then_inc(f_scores, 1)

                    def full_turn(n, half):
                        pe.wait_ge(f_norm, n + 1)
                        wait_for_bank(("turn", (n, half)))
                        for j in range(QT):
                            k = QT * half + j
                            last = nc.tensor.transpose(work[:, plan.bank["turn", (n, half)],
                                                            P * j:P * (j + 1)],
                                                       p_full[:, n % 2, P * k:P * (k + 1)], ident)
                        last.then_inc(f_turned, 1)

                    def full_value(s, half, k):
                        m = s - HEAD_STAGES
                        if k == 0:
                            copied = KT * m + (half + 1) * QT
                            pe.wait_ge(f_copied[0], copied)
                            pe.wait_ge(f_copied[1], copied)
                            pe.wait_ge(*taken("v1", s))
                            if 2 * m + half == 0:
                                pe.wait_ge(o_turned, ROUNDS)
                            else:
                                pe.wait_ge(f_out, 2 * m + half)
                        last = nc.tensor.matmul(outs[:, :], v_full[:, s % 2, k, :],
                                                pT_full[k // QT][:, k % QT, HALF * half:HALF * (half + 1)],
                                                start=k == 0, stop=k == KT - 1)
                        if k == KT - 1:
                            last.then_inc(f_pv, 1)

                    def value_biases():
                        pe.wait_ge(vectors_loaded, 16)
                        for layer, g in ((1, 0), (1, 1), (2, 0), (3, 0)):
                            column = 20 + (g if layer == 1 else layer)
                            last = nc.tensor.matmul(outs[:, layer:layer + 1], w_out(layer, g),
                                                    vec[:, column:column + 1],
                                                    start=g == 0, stop=layer > 1 or g == 1)
                        last.then_inc(value_bias, 1)

                    def do(kind, key):
                        if kind == "chunk":
                            chunk(*key)
                        elif kind == "tile":
                            score_tile(*key)
                        elif kind == "pair":
                            pair(key // 2, key % 2)
                        elif kind == "values" and key != -1:
                            values(key)
                        elif kind == "scores":
                            full_scores(key)
                        elif kind == "turn":
                            full_turn(*key)
                        elif kind == "value":
                            full_value(*key)

                    if not main:
                        pe.wait_ge(averages_loaded, 16)
                    for kind, key in plan.order:
                        do(kind, key)
                        if not main and (kind, key) == ("chunk", plan.FIRST[-1]):
                            value_biases()

            nc.all_engine_barrier(sems_to_clear=range(loop_sems[0].num, loop_sems[-1].num + 1))

        def image_at(tensor, n):
            return tensor[bass.ds(n, 1)].rearrange("o (p j) c -> (o p) j c", j=KT)

        def images(tensor, first):
            return [image_at(tensor, first + i) for i in range(PAIR)]

        run(Plan(main=False, then=True), images(x, 0), [])
        with nc.Fori(0, IMAGES // PAIR - 1) as step:
            run(Plan(main=True, then=True), images(x, step * PAIR + PAIR), images(out, step * PAIR))
        run(Plan(main=True, then=False), [], images(out, IMAGES - PAIR))


def kernel(**inputs):
    import numpy as np
    import concourse.bacc as _bacc
    from concourse import mybir as _mybir
    from concourse.bass_utils import run_bass_kernel_spmd as _run

    a = {n: np.asarray(v) for n, v in inputs.items()}
    C = CHANNELS

    def by_kind(w):
        return w.reshape(w.shape[0], HEADS, 3, HD).transpose(0, 2, 1, 3).reshape(w.shape[0], 3 * C)

    def padded(w):
        n = w.shape[1]
        rows = np.zeros((HEADS, 2 * HD, n), w.dtype)
        rows[:, :HD] = w.reshape(HEADS, HD, n)
        return rows.reshape(2, P, n).transpose(1, 0, 2).reshape(P, 2 * n)

    none = np.zeros((C,), np.float32)
    b1 = by_kind(a["L1_conv_b_qkv"][None])[0]
    weights = np.concatenate([
        by_kind(a["L0_conv_w_qkv"]), by_kind(a["L1_conv_w_qkv"]),
        a["L2_conv_Wq"], a["L2_conv_Wk"], a["L2_conv_Wv"],
        a["L3_conv_wq"], a["L3_conv_wk"], a["L3_conv_wv"],
        padded(a["L0_conv_w_out"]), padded(a["L1_conv_w_out"]),
        a["L2_conv_Wp"], a["L3_conv_wp"]], axis=1)
    vectors = np.stack([
        a["L0_conv_gn_scale"], a["L0_conv_gn_bias"], none, none, a["L0_conv_b_out"],
        a["L1_conv_gn_scale"], a["L1_conv_gn_bias"], b1[:C], b1[C:2 * C], a["L1_conv_b_out"],
        a["L2_conv_ln_g"], a["L2_conv_ln_b"], a["L2_conv_bq"], a["L2_conv_bk"], a["L2_conv_bp"],
        a["L3_conv_gamma"], a["L3_conv_beta"], a["L3_conv_bq"], a["L3_conv_bk"], a["L3_conv_bp"],
        *padded(b1[2 * C:, None]).T, a["L2_conv_bv"], a["L3_conv_bv"]],
        axis=1)
    block8 = np.kron(np.eye(C // 8), np.full((8, 8), 1 / 8)).astype(np.float32)
    block4 = np.kron(np.eye(C // 4), np.full((4, 4), 1 / 4)).astype(np.float32)
    averages = np.concatenate([block8, block4,
                               np.eye(C, dtype=np.float32)], axis=1)
    arrays = {"x": a["x"].reshape(IMAGES, TOKENS, C), "weights": weights, "vectors": vectors,
              "averages": averages}
    arrays = {n: np.ascontiguousarray(v) for n, v in arrays.items()}

    nc = _bacc.Bacc("TRN2", target_bir_lowering=False, num_devices=1)
    args = [nc.dram_tensor(n, v.shape, _mybir.dt.from_np(v.dtype), kind="ExternalInput").ap()
            for n, v in arrays.items()]
    out = nc.dram_tensor("out", (IMAGES, TOKENS, C), _mybir.dt.float32, kind="ExternalOutput").ap()
    attention_blocks(nc, *args, out)
    r = _run(nc, [arrays], core_ids=[0])
    return r.results[0]["out"].reshape(a["x"].shape)
```
